# Optimizing a Trainium2 kernel written in Bass

```python
import numpy as np
import jax
import jax.numpy as jnp

def _softmax(x, axis=-1):
    return jax.nn.softmax(x, axis=axis)

def _gelu(x):
    return jax.nn.gelu(x, approximate=True)

def _silu(x):
    return jax.nn.silu(x)

def _sigmoid(x):
    return jax.nn.sigmoid(x)

def _layernorm(x, axis=-1, eps=1e-05):
    m = jnp.mean(x, axis=axis, keepdims=True)
    v = jnp.var(x, axis=axis, keepdims=True)
    return (x - m) / jnp.sqrt(v + eps)

def _scatter_add(tgt, idx, src, axis=0):
    return tgt.at[idx].add(src)

def _segment_sum(src, seg, n):
    return jax.ops.segment_sum(src, seg, n)
kernel_name = 'mk_seq_postln_d1_jaxref_r4_ec762f'

def setup_inputs(seed: int=0):
    np.random.seed(seed)
    _w = jnp.asarray

    def _L0_attn_setup():
        import jax, jax.numpy as jnp
        import numpy as np
        B, T, HID = (4, 512, 256)
        H, DK, DV, K = (8, 64, 128, 4)
        EPS = 1e-05

        def _dw_causal_conv(x, w, b):
            xt = jnp.transpose(x, (0, 2, 1))
            y = jax.lax.conv_general_dilated(xt, w, window_strides=(1,), padding=[(K - 1, 0)], dimension_numbers=('NCH', 'OIH', 'NCH'), feature_group_count=x.shape[-1])
            y = y + b[None, :, None]
            return jnp.transpose(y, (0, 2, 1))

        def _forward(x, Wq, Wk, Wv, Wa, ba, Wb, bb, Wg, Wo, qc_w, qc_b, kc_w, kc_b, vc_w, vc_b, ln_w, ln_b):
            b, t = (x.shape[0], x.shape[1])
            scale = DK ** (-0.5)
            q = x @ Wq.T
            k = x @ Wk.T
            v = x @ Wv.T
            q = jax.nn.silu(_dw_causal_conv(q, qc_w, qc_b))
            k = jax.nn.silu(_dw_causal_conv(k, kc_w, kc_b))
            v = jax.nn.silu(_dw_causal_conv(v, vc_w, vc_b))
            q = q.reshape(b, t, H, DK)
            k = (k * scale).reshape(b, t, H, DK)
            v = v.reshape(b, t, H, DV)
            a = jax.nn.sigmoid(x @ Wa.T + ba).reshape(b, t, H, DV)
            beta = jax.nn.sigmoid(x @ Wb.T + bb)

            def step(S, ins):
                q_t, k_t, v_t, a_t, b_t = ins
                read = jnp.einsum('bhk,bhkv->bhv', k_t, S)
                err = read - v_t
                S = a_t[:, :, None, :] * S - b_t[:, :, None, None] * k_t[..., None] * err[:, :, None, :]
                o_t = jnp.einsum('bhk,bhkv->bhv', q_t, S)
                return (S, o_t)
            to_tbh = lambda u: jnp.moveaxis(u, 1, 0)
            S0 = jnp.zeros((b, H, DK, DV), x.dtype)
            _, o = jax.lax.scan(step, S0, (to_tbh(q), to_tbh(k), to_tbh(v), to_tbh(a), to_tbh(beta)))
            o = jnp.moveaxis(o, 0, 1)
            mu = jnp.mean(o, axis=-1, keepdims=True)
            var = jnp.mean((o - mu) ** 2, axis=-1, keepdims=True)
            o = (o - mu) * jax.lax.rsqrt(var + EPS) * ln_w + ln_b
            g = jax.nn.sigmoid(x @ Wg.T).reshape(b, t, H, DV)
            o = (o * g).reshape(b, t, H * DV)
            return o @ Wo.T
        key = jax.random.key(seed)
        ks = jax.random.split(key, 20)
        s = 0.02
        inp = {'x': jax.random.normal(ks[0], (B, T, HID), jnp.float32), 'Wq': jax.random.normal(ks[1], (H * DK, HID), jnp.float32) * s, 'Wk': jax.random.normal(ks[2], (H * DK, HID), jnp.float32) * s, 'Wv': jax.random.normal(ks[3], (H * DV, HID), jnp.float32) * s, 'Wa': jax.random.normal(ks[4], (H * DV, HID), jnp.float32) * s, 'ba': jax.random.normal(ks[5], (H * DV,), jnp.float32) * s, 'Wb': jax.random.normal(ks[6], (H, HID), jnp.float32) * s, 'bb': jax.random.normal(ks[7], (H,), jnp.float32) * s, 'Wg': jax.random.normal(ks[8], (H * DV, HID), jnp.float32) * s, 'Wo': jax.random.normal(ks[9], (HID, H * DV), jnp.float32) * s, 'qc_w': jax.random.normal(ks[10], (H * DK, 1, K), jnp.float32) * 0.3, 'qc_b': jnp.zeros((H * DK,), jnp.float32), 'kc_w': jax.random.normal(ks[11], (H * DK, 1, K), jnp.float32) * 0.3, 'kc_b': jnp.zeros((H * DK,), jnp.float32), 'vc_w': jax.random.normal(ks[12], (H * DV, 1, K), jnp.float32) * 0.3, 'vc_b': jnp.zeros((H * DV,), jnp.float32), 'ln_w': jnp.ones((DV,), jnp.float32), 'ln_b': jnp.zeros((DV,), jnp.float32)}
        return inp
    _L0_attn_in = _L0_attn_setup()

    def _L0_ffn_setup():
        import jax, jax.numpy as jnp
        import numpy as np
        B, S, D, F, E, NS, K = (2, 256, 256, 1024, 8, 8, 2)
        FS = F // NS
        key = jax.random.key(seed)
        ks = jax.random.split(key, 8)
        scale = 0.02
        return {'hidden_states': jax.random.normal(ks[0], (B, S, D), jnp.float32), 'gate_W': jax.random.normal(ks[1], (E, D), jnp.float32) * scale, 'w1_e': jax.random.normal(ks[2], (E, D, F), jnp.float32) * scale, 'w3_e': jax.random.normal(ks[3], (E, D, F), jnp.float32) * scale, 'w2_e': jax.random.normal(ks[4], (E, F, D), jnp.float32) * scale, 'w1_s': jax.random.normal(ks[5], (NS, D, FS), jnp.float32) * scale, 'w3_s': jax.random.normal(ks[6], (NS, D, FS), jnp.float32) * scale, 'w2_s': jax.random.normal(ks[7], (NS, FS, D), jnp.float32) * scale}
    _L0_ffn_in = _L0_ffn_setup()
    _d = {'L0_attn_x': _L0_attn_in['x'], 'L0_attn_Wq': _L0_attn_in['Wq'], 'L0_attn_Wk': _L0_attn_in['Wk'], 'L0_attn_Wv': _L0_attn_in['Wv'], 'L0_attn_Wa': _L0_attn_in['Wa'], 'L0_attn_ba': _L0_attn_in['ba'], 'L0_attn_Wb': _L0_attn_in['Wb'], 'L0_attn_bb': _L0_attn_in['bb'], 'L0_attn_Wg': _L0_attn_in['Wg'], 'L0_attn_Wo': _L0_attn_in['Wo'], 'L0_attn_qc_w': _L0_attn_in['qc_w'], 'L0_attn_qc_b': _L0_attn_in['qc_b'], 'L0_attn_kc_w': _L0_attn_in['kc_w'], 'L0_attn_kc_b': _L0_attn_in['kc_b'], 'L0_attn_vc_w': _L0_attn_in['vc_w'], 'L0_attn_vc_b': _L0_attn_in['vc_b'], 'L0_attn_ln_w': _L0_attn_in['ln_w'], 'L0_attn_ln_b': _L0_attn_in['ln_b'], 'L0_ffn_gate_W': _L0_ffn_in['gate_W'], 'L0_ffn_w1_e': _L0_ffn_in['w1_e'], 'L0_ffn_w3_e': _L0_ffn_in['w3_e'], 'L0_ffn_w2_e': _L0_ffn_in['w2_e'], 'L0_ffn_w1_s': _L0_ffn_in['w1_s'], 'L0_ffn_w3_s': _L0_ffn_in['w3_s'], 'L0_ffn_w2_s': _L0_ffn_in['w2_s']}
    _x0 = _d['L0_attn_x']
    _d['L0_attn_x'] = jax.random.normal(jax.random.fold_in(jax.random.key(seed), 1), (1, 4096, 256), dtype=_x0.dtype)
    del _x0
    return _d

def reference(L0_attn_x, L0_attn_Wq, L0_attn_Wk, L0_attn_Wv, L0_attn_Wa, L0_attn_ba, L0_attn_Wb, L0_attn_bb, L0_attn_Wg, L0_attn_Wo, L0_attn_qc_w, L0_attn_qc_b, L0_attn_kc_w, L0_attn_kc_b, L0_attn_vc_w, L0_attn_vc_b, L0_attn_ln_w, L0_attn_ln_b, L0_ffn_gate_W, L0_ffn_w1_e, L0_ffn_w3_e, L0_ffn_w2_e, L0_ffn_w1_s, L0_ffn_w3_s, L0_ffn_w2_s):

    def _L0_attn_ref(x, Wq, Wk, Wv, Wa, ba, Wb, bb, Wg, Wo, qc_w, qc_b, kc_w, kc_b, vc_w, vc_b, ln_w, ln_b):
        import jax, jax.numpy as jnp
        import numpy as np
        B, T, HID = (4, 512, 256)
        H, DK, DV, K = (8, 64, 128, 4)
        EPS = 1e-05

        def _dw_causal_conv(x, w, b):
            xt = jnp.transpose(x, (0, 2, 1))
            y = jax.lax.conv_general_dilated(xt, w, window_strides=(1,), padding=[(K - 1, 0)], dimension_numbers=('NCH', 'OIH', 'NCH'), feature_group_count=x.shape[-1])
            y = y + b[None, :, None]
            return jnp.transpose(y, (0, 2, 1))

        def _forward(x, Wq, Wk, Wv, Wa, ba, Wb, bb, Wg, Wo, qc_w, qc_b, kc_w, kc_b, vc_w, vc_b, ln_w, ln_b):
            b, t = (x.shape[0], x.shape[1])
            scale = DK ** (-0.5)
            q = x @ Wq.T
            k = x @ Wk.T
            v = x @ Wv.T
            q = jax.nn.silu(_dw_causal_conv(q, qc_w, qc_b))
            k = jax.nn.silu(_dw_causal_conv(k, kc_w, kc_b))
            v = jax.nn.silu(_dw_causal_conv(v, vc_w, vc_b))
            q = q.reshape(b, t, H, DK)
            k = (k * scale).reshape(b, t, H, DK)
            v = v.reshape(b, t, H, DV)
            a = jax.nn.sigmoid(x @ Wa.T + ba).reshape(b, t, H, DV)
            beta = jax.nn.sigmoid(x @ Wb.T + bb)

            def step(S, ins):
                q_t, k_t, v_t, a_t, b_t = ins
                read = jnp.einsum('bhk,bhkv->bhv', k_t, S)
                err = read - v_t
                S = a_t[:, :, None, :] * S - b_t[:, :, None, None] * k_t[..., None] * err[:, :, None, :]
                o_t = jnp.einsum('bhk,bhkv->bhv', q_t, S)
                return (S, o_t)
            to_tbh = lambda u: jnp.moveaxis(u, 1, 0)
            S0 = jnp.zeros((b, H, DK, DV), x.dtype)
            _, o = jax.lax.scan(step, S0, (to_tbh(q), to_tbh(k), to_tbh(v), to_tbh(a), to_tbh(beta)))
            o = jnp.moveaxis(o, 0, 1)
            mu = jnp.mean(o, axis=-1, keepdims=True)
            var = jnp.mean((o - mu) ** 2, axis=-1, keepdims=True)
            o = (o - mu) * jax.lax.rsqrt(var + EPS) * ln_w + ln_b
            g = jax.nn.sigmoid(x @ Wg.T).reshape(b, t, H, DV)
            o = (o * g).reshape(b, t, H * DV)
            return o @ Wo.T
        return _forward(x, Wq, Wk, Wv, Wa, ba, Wb, bb, Wg, Wo, qc_w, qc_b, kc_w, kc_b, vc_w, vc_b, ln_w, ln_b)

    def _L0_ffn_ref(hidden_states, gate_W, w1_e, w3_e, w2_e, w1_s, w3_s, w2_s):
        import jax, jax.numpy as jnp
        import numpy as np
        B, S, D, F, E, NS, K = (2, 256, 256, 1024, 8, 8, 2)
        FS = F // NS
        b, s, d = hidden_states.shape
        e = gate_W.shape[0]
        flat = hidden_states.reshape(-1, d)
        T = flat.shape[0]
        logits = (flat @ gate_W.T).astype(jnp.float32)
        probs = jax.nn.softmax(logits, axis=-1)
        top_v, top_i = jax.lax.top_k(probs, K)
        gates = jnp.zeros((T, e), probs.dtype).at[jnp.arange(T)[:, None], top_i].set(top_v)
        g = jax.nn.silu(jnp.einsum('td,edf->etf', flat, w1_e))
        u = jnp.einsum('td,edf->etf', flat, w3_e)
        out_e = jnp.einsum('etf,efd->etd', g * u, w2_e)
        routed = jnp.einsum('te,etd->td', gates, out_e).reshape(b, s, d)
        gs = jax.nn.silu(jnp.einsum('bsd,ndf->nbsf', hidden_states, w1_s))
        us = jnp.einsum('bsd,ndf->nbsf', hidden_states, w3_s)
        shared = jnp.einsum('nbsf,nfd->bsd', gs * us, w2_s) / w1_s.shape[0]
        alpha = 0.5
        return alpha * shared + (1.0 - alpha) * routed
    x = L0_attn_x
    x = _layernorm(x + _L0_attn_ref(x, L0_attn_Wq, L0_attn_Wk, L0_attn_Wv, L0_attn_Wa, L0_attn_ba, L0_attn_Wb, L0_attn_bb, L0_attn_Wg, L0_attn_Wo, L0_attn_qc_w, L0_attn_qc_b, L0_attn_kc_w, L0_attn_kc_b, L0_attn_vc_w, L0_attn_vc_b, L0_attn_ln_w, L0_attn_ln_b), axis=-1)
    x = _layernorm(x + _L0_ffn_ref(x, L0_ffn_gate_W, L0_ffn_w1_e, L0_ffn_w3_e, L0_ffn_w2_e, L0_ffn_w1_s, L0_ffn_w3_s, L0_ffn_w2_s), axis=-1)
    return x

_drawn_inputs = setup_inputs


def setup_inputs(seed=0):
    import zlib

    import numpy as np

    out = dict(_drawn_inputs(seed))
    spreads = {'L0_attn_qc_b': (0.0, 0.1),
     'L0_attn_kc_b': (0.0, 0.1),
     'L0_attn_vc_b': (0.0, 0.1),
     'L0_attn_ln_w': (1.0, 0.6),
     'L0_attn_ln_b': (0.0, 0.1)}
    factors = {'L0_attn_Wa': 7.281,
     'L0_attn_ba': 8.0,
     'L0_attn_Wb': 4.973,
     'L0_attn_bb': 8.0,
     'L0_attn_Wg': 4.076,
     'L0_ffn_gate_W': 8.0,
     'L0_ffn_w1_e': 8.0,
     'L0_ffn_w3_e': 8.0,
     'L0_ffn_w2_e': 8.0,
     'L0_ffn_w1_s': 8.0,
     'L0_ffn_w3_s': 8.0,
     'L0_ffn_w2_s': 8.0}
    for name, (base, spread) in spreads.items():
        noise = np.random.default_rng([zlib.crc32(name.encode()), seed]).standard_normal(out[name].shape)
        drawn = base * np.exp(spread * noise) if base else spread * noise
        out[name] = jnp.asarray(drawn.astype(out[name].dtype))
    for name, factor in factors.items():
        out[name] = (out[name] * factor).astype(out[name].dtype)
    return out
```

```python
from contextlib import ExitStack

import numpy as np
import concourse.bass as bass
from concourse import mybir

F32 = mybir.dt.float32
ALU = mybir.AluOpType
ACT = mybir.ActivationFunctionType
X = mybir.AxisListType.X
ds = bass.ds

T, D = 4096, 256
H, DK, DV, KC = 8, 64, 128, 4
PR = H // 2
P = 128
DC = D // P
TT = 512
NT = T // TT
CH = 8
NC = TT // CH
SL = CH + 1
E, FF = 8, 1024
NE = E + 1
FB = FF // P
SUB = TT // P
EPS = 1e-5
SCALE = float(DK) ** -0.5
NF = 8 + 4 + 4 + 8
CREDIT = 2


def attention(nc, io, dram, gates_all):
    ctx = ExitStack()
    with ctx:
        def sb(name, shape):
            return ctx.enter_context(nc.sbuf_tensor(name, shape, F32))

        def sem(name):
            return ctx.enter_context(nc.semaphore(name))

        wq, wk = sb("wq", [P, DC, H * DK]), sb("wk", [P, DC, H * DK])
        wv, wa, wg = (sb(n, [P, DC, H * DV]) for n in ("wv", "wa", "wg"))
        wo = sb("wo", [P, H, D])
        wb = sb("wb", [P, DC, H])
        gw = sb("gw", [P, DC, E])
        taps = sb("taps", [P, 16, KC + 1])
        ba = sb("ba", [P, H])
        bb = sb("bb", [H, 1])
        lnwb = sb("lnwb", [P, 2])
        ident, mean_w = (sb(n, [P, P]) for n in ("ident", "mean_w"))
        half_ones = sb("half_ones", [P, 2, P])
        sel_v = sb("sel_v", [H, H, P])
        sel_p = sb("sel_p", [H, PR, P])
        lower = sb("lower", [P, E * E])
        eps = sb("eps", [P, 1])
        xT = sb("xT", [P, DC, TT])
        xt = sb("xt", [P, SUB, D])
        a = sb("a", [P, H, TT])
        bv = sb("bv", [P, H, TT])
        K = sb("K", [P, PR, TT])
        QK = sb("QK", [P, PR, 2, TT])
        oT = sb("oT", [P, H, TT])
        halo = sb("halo", [P, 16, KC - 1])
        raw = sb("raw", [P, 2, KC - 1 + TT])
        acc = sb("acc", [P, 2, TT])
        sil = sb("sil", [P, 2, TT])
        beta = sb("beta", [H, TT])
        R = sb("R", [P, 2, H, SL, SL])
        W = sb("W", [P, 2, H, 72])
        INV = sb("INV", [P, 2, H, 2, 16])
        inv_tmp = sb("inv_tmp", [P, H, 2, 3])
        prod_k = sb("prod_k", [P, PR, CH, CH])
        prod_q = sb("prod_q", [P, PR, CH, CH])
        kexp = sb("kexp", [P, 288])
        qkx = sb("qkx", [P, 2, PR, 2, 2, CH])
        Krow = sb("Krow", [H * CH, 2, PR, P])
        gq = sb("gq", [P, H, CH, CH])
        Nq = sb("Nq", [P, 2, H, CH, CH])
        rq = sb("rq", [P, H, CH])
        tree = sb("tree", [P, H, CH, 8])
        rsc = sb("rsc", [P, H, CH])
        c_in = sb("c_in", [P, H, CH])
        c_lo = sb("c_lo", [P, H, 4])
        P1 = sb("P1", [P, H, 4, 4])
        P2 = sb("P2", [P, H, 4, 5])
        c_hi = sb("c_hi", [P, H, 4])
        U = sb("U", [P, 2, H, CH])
        uF = sb("uF", [P, P])
        uT = sb("uT", [H * CH, P])
        dT = sb("dT", [H, P])
        S = sb("S", [P, 2, PR, P])
        SD = sb("SD", [P, PR, P])
        sq = acc
        sd = sil
        gt = raw
        x1 = sb("x1", [P, 2, D])
        x1T = sb("x1T", [P, 2, DC, P])
        stat = sb("stat", [P, 16])
        L = sb("L", [P, SUB, E])
        big = sb("big", [P, SUB, E, E])
        big2 = sb("big2", [P, SUB, E, E])
        small = sb("small", [P, 4, SUB])
        Lp = sb("Lp", [P, SUB, E])

        bank = [ctx.enter_context(nc.psum_tensor(f"bank{i}", [P, 512], F32)) for i in range(8)]
        g_k = bank[0][:, :].rearrange("p (h t j) -> p h t j", h=H, t=CH)
        g_q = bank[1][:, :].rearrange("p (h t j) -> p h t j", h=H, t=CH)
        k_row = bank[2][0:64, :].rearrange("p (r k) -> p r k", r=PR)
        upd = bank[3][:, :].rearrange("p (r v) -> p r v", r=PR)
        dbc = bank[4][:, :].rearrange("p (r v) -> p r v", r=PR)
        read = bank[5][:, 0:128].rearrange("p (h x t) -> p h x t", h=H, x=2)
        read_p = bank[5][:, 0:128].rearrange("p (g r y) -> p r g y", g=2, r=PR)
        u_row = bank[6][:, 0:P]
        d_row = bank[7][0:H, 0:P]

        R81 = R[:, :, :, :, :].rearrange("p b h s r -> p b h (s r)")
        W64 = W[:, :, :, 0:64].rearrange("p b h (t j) -> p b h t j", t=CH)
        W36 = W[:, :, :, :].rearrange("p b h (k r) -> p b h k r", k=2)
        kexp64 = kexp[:, 0:256].rearrange("p (r c) -> p r c", r=PR)
        kexp72 = kexp[:, :].rearrange("p (r c) -> p r c", c=72)

        loaded = sem("loaded")
        ready_set = sem("ready_set")
        xT_in = sem("xT_in")
        xt_in = sem("xt_in")
        stored = [sem(f"stored{i}") for i in range(2)]
        beta_logit = sem("beta_logit")
        beta_sig = sem("beta_sig")
        projected = sem("projected")
        evacuated = sem("evacuated")
        raw_in = sem("raw_in")
        tap = sem("tap")
        halo_in = sem("halo_in")
        conv_done = sem("conv_done")
        silu_done = sem("silu_done")
        beta_bc = sem("beta_bc")
        beta_used = sem("beta_used")
        key_step = sem("key_step")
        tile_in = sem("tile_in")
        names = ("slots_in", "rq_in", "qkx_in", "kexp_in", "krow_in", "gq_in", "ut_in", "dt_in",
                 "slots_used", "prodk", "prodq", "w_in", "sd_in", "u_in", "uf_in", "state_in", "cin_used",
                 "gramk", "gramq", "krow_ps", "reads_ps", "ut_ps", "dt_ps", "dbc_ps", "upd_ps",
                 "nq_in", "o_in", "rs_in", "decays_in", "inv_in", "c_in_s")
        s = {n: sem("s_" + n) for n in names}
        decay_step = sem("decay_step")
        inv_step = sem("inv_step")
        sub_step = sem("sub_step")
        out_step = sem("out_step")
        mean_ps, centred, squared, var_ps, sd_in, normed = (sem(n) for n in (
            "mean_ps", "centred", "squared", "var_ps", "sd_root", "normed"))
        rstd_in = sem("rstd_in")
        gate_ps, gate_in, affine, gated = (sem(n) for n in ("gate_ps", "gate_in", "affine", "gated"))
        y_ps, resid, ln_step, ln_root, x1_in = (sem(n) for n in ("y_ps", "resid", "ln_step", "ln_root", "x1_in"))
        xT_ps, x1T_in, logit_ps = (sem(n) for n in ("xT_ps", "x1T_in", "logit_ps"))
        route_step, route_max, route_exp, routed = (sem(n) for n in ("route_step", "route_max", "route_exp", "routed"))

        block = ctx.enter_context(nc.Block())
        n_loads = len(io["const_loads"])
        consts = dict(wq=wq, wk=wk, wv=wv, wa=wa, wg=wg, wo=wo, wb=wb, gw=gw, taps=taps, ba=ba, bb=bb,
                      lnwb=lnwb, ident=ident, half_ones=half_ones, mean_w=mean_w, sel_v=sel_v, sel_p=sel_p,
                      lower=lower, eps=eps)

        def chunk_loop(eng, tile, first, step):
            first(tile * NC, 0, 0)
            with eng.Fori(0, NC // 2 - 1) as i:
                for b in range(2):
                    step(tile * NC + i * 2 + b, i * 2 + b, b, 2)
            step(tile * NC + NC - 2, NC - 2, 0, 1)
            step(tile * NC + NC - 1, NC - 1, 1, 0)

        @block.sync
        def _(sp):
            for name in io["const_loads"]:
                t = consts[name]
                sp.dma_start(t.ap(), io[name]).then_inc(loaded, 16)
            for b in range(2):
                sp.sem_inc(stored[b], 32)
            with sp.Fori(0, NT) as tile:
                sp.wait_ge(gate_ps, tile * H + 1)
                sp.dma_start(xT[:, :, :], io["xT"][:, :, ds(tile * TT, TT)]).then_inc(xT_in, 16)
                sp.dma_start(xt[:, :, :], io["x"][:, ds(tile * SUB, SUB), :]).then_inc(xt_in, 16)
                for q in range(SUB):
                    sp.wait_ge(x1_in, tile * SUB + q + 1)
                    sp.dma_start(dram["x1"][:, ds(tile * SUB + q, 1), :], x1[:, q % 2:q % 2 + 1, :]).then_inc(stored[q % 2], 16)
                    sp.wait_ge(x1T_in, tile * SUB + q + 1)
                    sp.dma_start(dram["x1T"][:, :, ds(tile * TT + q * P, P)], x1T[:, q % 2, :, :]).then_inc(stored[q % 2], 16)
            for b in range(2):
                sp.wait_ge(stored[b], 32 * (NT * SUB // 2 + 1))

        @block.gpsimd
        def _(pool):
            for t in (kexp[:, :], qkx[:, :, :, :, :, :], halo[:, :, :], S[:, :, :, :], INV[:, :, :, :, :], uF[:, :]):
                pool.memset(t, 0.0).then_inc(ready_set, 1)
            pool.memset(R81[:, :, :, :], 0.0).then_inc(ready_set, 1)
            pool.wait_ge(ready_set, 7)
            pool.memset(R81[:, :, :, 0:81:10], 1.0).then_inc(ready_set, 1)
            pool.memset(INV[:, :, :, :, 0:16:5], 1.0).then_inc(ready_set, 1)
            pool.wait_ge(ready_set, 9)

            def weigh(n, c, b):
                pool.wait_ge(s["gq_in"], n + 1 + CREDIT)
                pool.wait_ge(s["decays_in"], n + 1 + CREDIT)
                pool.tensor_tensor(Nq[:, b], gq[:, :, :, :],
                                   R[:, b, :, 1:SL, 1:SL].rearrange("p h j t -> p h t j"), ALU.mult)\
                    .then_inc(s["nq_in"], 1)

            def outputs(n, c, b):
                pool.wait_ge(s["rq_in"], n + 1 + CREDIT)
                pool.wait_ge(s["o_in"], n + CREDIT)
                pool.tensor_tensor(rsc[:, :, :], rq[:, :, :], R[:, b, :, 0, 1:SL], ALU.mult).then_inc(s["rs_in"], 1)
                pool.wait_ge(s["u_in"], n + 1 + CREDIT)
                pool.wait_ge(s["nq_in"], n + 1 + CREDIT)
                pool.tensor_tensor(Nq[:, b], Nq[:, b],
                                   U[:, b].unsqueeze(2).to_broadcast([P, H, CH, CH]), ALU.mult).then_inc(out_step, 1)
                pool.wait_ge(out_step, n * 4 + 1 + CREDIT * 4)
                pool.tensor_tensor(tree[:, :, :, 0:4], Nq[:, b, :, :, 0:4], Nq[:, b, :, :, 4:8], ALU.add).then_inc(out_step, 1)
                pool.wait_ge(out_step, n * 4 + 2 + CREDIT * 4)
                pool.tensor_tensor(tree[:, :, :, 4:6], tree[:, :, :, 0:2], tree[:, :, :, 2:4], ALU.add).then_inc(out_step, 1)
                pool.wait_ge(out_step, n * 4 + 3 + CREDIT * 4)
                pool.wait_ge(s["rs_in"], n + 1 + CREDIT)
                pool.tensor_tensor(tree[:, :, :, 6], tree[:, :, :, 4], tree[:, :, :, 5], ALU.add).then_inc(out_step, 1)
                pool.wait_ge(out_step, n * 4 + 4 + CREDIT * 4)
                pool.tensor_tensor(oT[:, :, ds(c * CH, CH)], tree[:, :, :, 6], rsc[:, :, :], ALU.add).then_inc(s["o_in"], 1)

            def step(n, c, b, left):
                outputs(n, c, b)
                if left:
                    weigh(n + 1, c + 1, 1 - b)

            pool.sem_inc(out_step, 4 * CREDIT)
            for name in ("nq_in", "rs_in", "o_in"):
                pool.sem_inc(s[name], CREDIT)
            with pool.Fori(0, NT) as tile:
                pool.wait_ge(gated, tile * H + 2)
                pool.wait_ge(y_ps, tile * SUB + 1)
                chunk_loop(pool, tile, weigh, step)

        @block.scalar
        def _(act):
            def conv_part(tile, f):
                e = 8 + f
                act.wait_ge(projected, tile * NF + e + 1)
                act.wait_ge(conv_done, tile * 16 + f - 1 + 2)
                act.wait_ge(silu_done, tile * 16 + f - 1 + 2)
                act.copy(raw[:, f % 2, KC - 1:], bank[e % 2][:, :]).then_inc(raw_in, 1)
                act.activation(acc[:, f % 2, :], bank[e % 2][:, :], ACT.Identity, bias=taps[:, f, KC:KC + 1],
                               scale=taps[:, f, KC - 1:KC]).then_inc(evacuated, 1)

            def silu_part(tile, f):
                act.wait_ge(conv_done, tile * 16 + f + 1 + 2)
                if f >= 4:
                    act.wait_ge(beta_used, tile * 12 + f - 4 - 1 + 2)
                dst = QK[:, f, 1, :] if f < 4 else sil[:, f % 2, :]
                act.activation(dst, acc[:, f % 2, :], ACT.Silu).then_inc(silu_done, 1)

            def prepare(n, c, b):
                act.wait_ge(s["uf_in"], n - 1 + CREDIT)
                act.wait_ge(s["dt_ps"], n - 1 + CREDIT)
                act.wait_ge(s["rs_in"], n - 1 + CREDIT)
                act.wait_ge(s["w_in"], n - 1 + CREDIT)
                act.copy(R81[:, b, :, 1:72:10], a[:, :, ds(c * CH, CH)]).then_inc(s["slots_in"], 1)

            def stage(n, c, b):
                act.wait_ge(s["reads_ps"], n - 1 + CREDIT)
                for half in range(2):
                    r = slice(64 * half, 64 * half + 64)
                    i = act.copy(qkx[r, b, :, half, :, :], QK[r, :, :, ds(c * CH, CH)])
                i.then_inc(s["qkx_in"], 1)
                act.wait_ge(s["krow_ps"], n + CREDIT)
                for half in range(2):
                    r = slice(64 * half, 64 * half + 64)
                    i = act.copy(kexp72[r, :, 32 * half:32 * half + CH], K[r, :, ds(c * CH, CH)])
                i.then_inc(s["kexp_in"], 1)

            def finish(n, c, b):
                act.wait_ge(s["dt_ps"], n + 1 + CREDIT)
                act.wait_ge(s["dbc_ps"], n + CREDIT)
                act.copy(dT[:, :], d_row).then_inc(s["dt_in"], 1)
                act.wait_ge(s["krow_ps"], n + 1 + CREDIT)
                act.wait_ge(s["upd_ps"], n - 1 + CREDIT)
                act.copy(Krow[:, b], k_row).then_inc(s["krow_in"], 1)
                act.wait_ge(s["gramq"], n + 1 + CREDIT)
                act.wait_ge(s["nq_in"], n + CREDIT)
                act.copy(gq[:, :, :, :], g_q).then_inc(s["gq_in"], 1)

            def first(n, c, b):
                prepare(n, c, b)
                stage(n, c, b)
                finish(n, c, b)
                prepare(n + 1, c + 1, 1 - b)

            def step(n, c, b, left):
                act.wait_ge(s["c_in_s"], n + 1 + CREDIT)
                act.wait_ge(s["rs_in"], n + CREDIT)
                act.copy(rq[:, :, :], read[:, :, 1, :]).then_inc(s["rq_in"], 1)
                if left:
                    stage(n + 1, c + 1, 1 - b)
                act.wait_ge(s["ut_ps"], n + 1 + CREDIT)
                act.wait_ge(s["upd_ps"], n + CREDIT)
                act.copy(uT[:, :], u_row[0:H * CH, :]).then_inc(s["ut_in"], 1)
                if left:
                    finish(n + 1, c + 1, 1 - b)
                if left == 2:
                    prepare(n + 2, c + 2, b)

            act.wait_ge(loaded, 16 * n_loads)
            act.wait_ge(ready_set, 9)
            for name in ("slots_in", "rq_in", "qkx_in", "kexp_in", "krow_in", "gq_in", "ut_in", "dt_in"):
                act.sem_inc(s[name], CREDIT)
            act.sem_inc(silu_done, 2)
            with act.Fori(0, NT) as tile:
                act.wait_ge(beta_logit, tile + 1)
                act.activation(beta[:, :], bank[4][0:H, :], ACT.Sigmoid, bias=bb[:, :]).then_inc(beta_sig, 1)
                for e in range(H):
                    act.wait_ge(projected, tile * NF + e + 1)
                    act.activation(a[:, e, :], bank[e % 2][:, :], ACT.Sigmoid, bias=ba[:, e:e + 1]).then_inc(evacuated, 1)
                for f in range(16):
                    conv_part(tile, f)
                    if f:
                        silu_part(tile, f - 1)
                silu_part(tile, 15)
                act.wait_ge(tile_in, tile + 1)
                act.wait_ge(silu_done, tile * 16 + 16 + 2)
                chunk_loop(act, tile, first, step)
                for h in range(H):
                    act.wait_ge(centred, tile * H + h + 1)
                    act.wait_ge(var_ps, tile * H + h - 1 + 2)
                    act.activation(sq[:, h % 2, :], oT[:, h, :], ACT.Square).then_inc(squared, 1)
                    act.wait_ge(var_ps, tile * H + h + 1 + 2)
                    act.wait_ge(rstd_in, tile * H + h - 1 + 2)
                    act.activation(sd[:, h % 2, :], bank[2 + h % 2][:, :], ACT.Sqrt, bias=eps[:, :]).then_inc(sd_in, 1)
                for h in range(H):
                    act.wait_ge(gate_ps, tile * H + h + 1 + 1)
                    act.wait_ge(gated, tile * H + h - 1 + 2)
                    act.activation(gt[:, h % 2, 0:TT], bank[4 + h % 2][:, :], ACT.Sigmoid).then_inc(gate_in, 1)
                for q in range(SUB):
                    act.wait_ge(ln_step, (tile * SUB + q) * 4 + 2)
                    act.activation(stat[:, 10:11], stat[:, 7:8], ACT.Sqrt, bias=eps[:, :]).then_inc(ln_root, 1)
                    act.wait_ge(xT_ps, tile * SUB + q + 1 + 2)
                    act.wait_ge(stored[q % 2], 32 * (tile * 2 + q // 2 + 1))
                    act.wait_ge(logit_ps, tile * SUB + q - 1 + 2)
                    act.copy(x1T[:, q % 2], bank[0][:, 0:D].rearrange("p (c t) -> p c t", c=DC)).then_inc(x1T_in, 1)
                act.wait_ge(route_max, tile + 1)
                act.activation(Lp[:, :, :], L[:, :, :], ACT.Exp).then_inc(route_exp, 1)

        @block.tensor
        def _(pe):
            mm, tr = pe.matmul, pe.transpose

            def project(out, w, e):
                for c in range(DC):
                    i = mm(out, w[:, c, e * P:(e + 1) * P], xT[:, c, :], start=c == 0, stop=c == DC - 1)
                return i

            def grams(n, c, b):
                for ps, prod, made, done, used in ((g_k, prod_k, "prodk", "gramk", "w_in"),
                                                  (g_q, prod_q, "prodq", "gramq", "gq_in")):
                    pe.wait_ge(s[made], n + 1 + CREDIT)
                    pe.wait_ge(s[used], n + CREDIT)
                    for half in range(2):
                        i = mm(ps[:, 4 * half:4 * half + 4], half_ones[:, half, :], prod[:, :, :, :], start=True, stop=True)
                    i.then_inc(s[done], 1)

            def key_rows(n, c, b):
                for p in range(PR):
                    i = tr(k_row[:, p, :], kexp64[:, p, :], ident[:, :])
                i.then_inc(s["krow_ps"], 1)

            def decay_row(n, c, b):
                pe.wait_ge(s["kexp_in"], n + 1 + CREDIT)
                pe.wait_ge(s["krow_in"], n + CREDIT)
                pe.wait_ge(s["decays_in"], n + 1 + CREDIT)
                pe.wait_ge(s["dt_in"], n + CREDIT)
                tr(d_row, R[:, b, :, 0, CH], ident[:, :]).then_inc(s["dt_ps"], 1)

            def decay_bc(n, c, b):
                pe.wait_ge(s["dt_in"], n + 1 + CREDIT)
                pe.wait_ge(s["sd_in"], n + CREDIT)
                for p in range(PR):
                    i = mm(dbc[:, p, :], sel_p[:, p, :], dT[:, :], start=True, stop=True)
                i.then_inc(s["dbc_ps"], 1)

            def first(n, c, b):
                grams(n, c, b)
                decay_row(n, c, b)
                key_rows(n, c, b)
                decay_bc(n, c, b)

            def step(n, c, b, left):
                pe.wait_ge(s["state_in"], n + CREDIT)
                pe.wait_ge(s["qkx_in"], n + 1 + CREDIT)
                pe.wait_ge(s["rq_in"], n + CREDIT)
                pe.wait_ge(s["c_in_s"], n + CREDIT)
                for p in range(PR):
                    i = mm(read_p[:, p], S[:, b, p, :], qkx[:, b, p].rearrange("p g x t -> p (g x t)"), start=True, stop=True)
                i.then_inc(s["reads_ps"], 1)
                if left:
                    grams(n + 1, c + 1, 1 - b)
                pe.wait_ge(s["uf_in"], n + 1 + CREDIT)
                pe.wait_ge(s["ut_in"], n + CREDIT)
                tr(u_row, uF[:, :], ident[:, :]).then_inc(s["ut_ps"], 1)
                if left:
                    decay_row(n + 1, c + 1, 1 - b)
                pe.wait_ge(s["ut_in"], n + 1 + CREDIT)
                pe.wait_ge(s["krow_in"], n + 1 + CREDIT)
                pe.wait_ge(s["state_in"], n + CREDIT)
                for p in range(PR):
                    i = mm(upd[:, p, :], Krow[:, b, p, :], uT[:, :], start=True, stop=True)
                i.then_inc(s["upd_ps"], 1)
                if left:
                    key_rows(n + 1, c + 1, 1 - b)
                    decay_bc(n + 1, c + 1, 1 - b)

            pe.wait_ge(loaded, 16 * n_loads)
            pe.wait_ge(ready_set, 9)
            for name in ("gramk", "gramq", "krow_ps", "reads_ps", "ut_ps", "dt_ps", "dbc_ps", "upd_ps"):
                pe.sem_inc(s[name], CREDIT)
            pe.sem_inc(gate_ps, 1)
            pe.sem_inc(y_ps, 1)
            pe.sem_inc(var_ps, 2)
            pe.sem_inc(xT_ps, 2)
            pe.sem_inc(logit_ps, 2)
            with pe.Fori(0, NT) as tile:
                pe.wait_ge(xT_in, 16 * tile + 16)
                pe.wait_ge(routed, tile + 1)
                for c in range(DC):
                    i = mm(bank[4][0:H, :], wb[:, c, :], xT[:, c, :], start=c == 0, stop=c == DC - 1)
                i.then_inc(beta_logit, 1)
                parts = [(wa, h) for h in range(H)] + [(wq, p) for p in range(PR)] + [(wk, p) for p in range(PR)]\
                    + [(wv, h) for h in range(H)]
                for e, (w, j) in enumerate(parts):
                    if e >= 2:
                        pe.wait_ge(evacuated, tile * NF + e - 1)
                    project(bank[e % 2][:, :], w, j).then_inc(projected, 1)
                    if e >= 12:
                        j = e - 12
                        if j == 0:
                            pe.wait_ge(beta_sig, tile + 1)
                        pe.wait_ge(beta_used, tile * 12 + j - 1 + 2)
                        sel = sel_p[:, j, :] if j < PR else sel_v[:, j - PR, :]
                        mm(bank[2 + j % 2][:, :], sel, beta[:, :], start=True, stop=True).then_inc(beta_bc, 1)
                pe.wait_ge(evacuated, tile * NF + NF)
                pe.wait_ge(tile_in, tile + 1)
                chunk_loop(pe, tile, first, step)
                pe.wait_ge(s["o_in"], tile * NC + NC + CREDIT)
                pe.wait_ge(s["state_in"], tile * NC + NC + CREDIT)

                def variance(h):
                    pe.wait_ge(squared, tile * H + h + 1)
                    pe.wait_ge(sd_in, tile * H + h - 1 + 2)
                    mm(bank[2 + h % 2][:, :], mean_w[:, :], sq[:, h % 2, :], start=True, stop=True).then_inc(var_ps, 1)
                for h in range(H):
                    if h >= 2:
                        pe.wait_ge(centred, tile * H + h - 1)
                    mm(bank[h % 2][:, :], mean_w[:, :], oT[:, h, :], start=True, stop=True).then_inc(mean_ps, 1)
                    if h:
                        variance(h - 1)
                variance(H - 1)
                for h in range(H):
                    if h >= 2:
                        pe.wait_ge(gate_in, tile * H + h - 1)
                    project(bank[4 + h % 2][:, :], wg, h).then_inc(gate_ps, 1)

                def transposes(q):
                    pe.wait_ge(x1_in, tile * SUB + q + 1)
                    if q:
                        pe.wait_ge(x1T_in, tile * SUB + q)
                    else:
                        pe.wait_ge(normed, tile + 1)
                    for c in range(DC):
                        i = tr(bank[0][:, c * P:(c + 1) * P], x1[:, q % 2, c * P:(c + 1) * P], ident[:, :])
                    i.then_inc(xT_ps, 1)

                def logits(q):
                    pe.wait_ge(x1T_in, tile * SUB + q + 1)
                    for c in range(DC):
                        i = mm(bank[1][:, q * E:(q + 1) * E], x1T[:, q % 2, c, :], gw[:, c, :], start=c == 0, stop=c == DC - 1)
                    i.then_inc(logit_ps, 1)
                pe.wait_ge(gated, tile * H + H + 2)
                for q in range(SUB):
                    if q >= 2:
                        pe.wait_ge(resid, tile * SUB + q - 1 + 1)
                    for h in range(H):
                        i = mm(bank[6 + q % 2][:, 0:D], oT[:, h, q * P:(q + 1) * P], wo[:, h, :], start=h == 0, stop=h == H - 1)
                    i.then_inc(y_ps, 1)
                for q in range(SUB):
                    transposes(q)
                    logits(q)

        @block.vector
        def _(dve):
            tt, stt = dve.tensor_tensor, dve.scalar_tensor_tensor

            def conv(tile, f):
                b = f % 2
                dve.tensor_copy(raw[:, b, 0:KC - 1], halo[:, f, :]).then_inc(halo_in, 1)
                dve.wait_ge(halo_in, tile * 16 + f + 1)
                dve.wait_ge(raw_in, tile * 16 + f + 1)
                dve.wait_ge(evacuated, tile * NF + 8 + f + 1)
                for k in range(KC - 1):
                    if k:
                        dve.wait_ge(tap, tile * 48 + 3 * f + k)
                    i = stt(acc[:, b, :], raw[:, b, k:k + TT], taps[:, f, k:k + 1], acc[:, b, :], ALU.mult, ALU.add)
                    i.then_inc(tap, 1)
                dve.wait_ge(tap, tile * 48 + 3 * f + 3)
                dve.tensor_copy(halo[:, f, :], raw[:, b, TT:]).then_inc(conv_done, 1)

            def use_beta(tile, f):
                j = f - 4
                dve.wait_ge(silu_done, tile * 16 + f + 1 + 2)
                dve.wait_ge(beta_bc, tile * 12 + j + 1)
                ps = bank[2 + j % 2][:, :]
                if j < PR:
                    dve.tensor_scalar(K[:, j, :], sil[:, f % 2, :], SCALE, None, ALU.mult).then_inc(key_step, 1)
                    stt(QK[:, j, 0, :], sil[:, f % 2, :], -SCALE, ps, ALU.mult, ALU.mult).then_inc(beta_used, 1)
                else:
                    tt(bv[:, j - PR, :], sil[:, f % 2, :], ps, ALU.mult).then_inc(beta_used, 1)

            def decays_a(n, c, b):
                dve.wait_ge(s["slots_in"], n + 1 + CREDIT)
                tt(R81[:, b, :, 2:63:20], R81[:, b, :, 1:62:20], R81[:, b, :, 11:72:20], ALU.mult).then_inc(decay_step, 1)

            def decays_b(n, c, b):
                dve.wait_ge(decay_step, n * 3 + 1)
                for o in (0, 4):
                    tt(R[:, b, :, o:o + 2, o + 3:o + 5], R[:, b, :, o:o + 2, o + 2:o + 3].to_broadcast([P, H, 2, 2]),
                       R[:, b, :, o + 2:o + 3, o + 3:o + 5].to_broadcast([P, H, 2, 2]), ALU.mult).then_inc(decay_step, 1)

            def decays_c(n, c, b):
                dve.wait_ge(decay_step, n * 3 + 3)
                tt(R[:, b, :, 0:4, 5:9], R[:, b, :, 0:4, 4:5].to_broadcast([P, H, 4, 4]),
                   R[:, b, :, 4:5, 5:9].to_broadcast([P, H, 4, 4]), ALU.mult).then_inc(s["decays_in"], 1)

            def products(n, c, b, x, out, made, used):
                dve.wait_ge(s[used], n + CREDIT)
                tok = ds(c * CH, CH)
                tt(out[:, :, :, :], QK[:, :, x, tok].unsqueeze(3).to_broadcast([P, PR, CH, CH]),
                   K[:, :, tok].unsqueeze(2).to_broadcast([P, PR, CH, CH]), ALU.mult).then_inc(s[made], 1)

            def weights(n, c, b):
                dve.wait_ge(s["gramk"], n + 1 + CREDIT)
                dve.wait_ge(s["decays_in"], n + 1 + CREDIT)
                tt(W64[:, b, :, 1:8, 0:7], g_k[:, :, 1:8, 0:7], R[:, b, :, 1:8, 1:8].rearrange("p h j t -> p h t j"),
                   ALU.mult).then_inc(s["w_in"], 1)

            def inverses(n, c, b):
                w, v, m = W36[:, b], INV[:, b], inv_tmp
                dve.wait_ge(s["w_in"], n + 1 + CREDIT)
                dve.tensor_copy(v[:, :, :, 4:15:5], w[:, :, :, 8:27:9]).then_inc(inv_step, 1)
                tt(m[:, :, :, 0:2], w[:, :, :, 17:27:9], w[:, :, :, 8:18:9], ALU.mult).then_inc(inv_step, 1)
                dve.wait_ge(inv_step, n * 5 + 2)
                tt(v[:, :, :, 8:14:5], m[:, :, :, 0:2], w[:, :, :, 16:26:9], ALU.add).then_inc(inv_step, 1)
                dve.wait_ge(inv_step, n * 5 + 3)
                tt(m[:, :, :, 0:2], w[:, :, :, 25:27], v[:, :, :, 4:9:4], ALU.mult).then_inc(inv_step, 1)
                dve.wait_ge(inv_step, n * 5 + 4)
                tt(m[:, :, :, 2], m[:, :, :, 0], m[:, :, :, 1], ALU.add).then_inc(inv_step, 1)
                dve.wait_ge(inv_step, n * 5 + 5)
                tt(v[:, :, :, 12], m[:, :, :, 2], w[:, :, :, 24], ALU.add).then_inc(s["inv_in"], 1)

            def first(n, c, b):
                decays_a(n, c, b)
                products(n, c, b, 0, prod_k, "prodk", "gramk")
                decays_b(n, c, b)
                products(n, c, b, 1, prod_q, "prodq", "gramq")
                decays_c(n, c, b)
                weights(n, c, b)
                inverses(n, c, b)
                products(n + 1, c + 1, b, 0, prod_k, "prodk", "gramk")
                products(n + 1, c + 1, b, 1, prod_q, "prodq", "gramq")

            def step(n, c, b, left):
                at = lambda k: n * 7 + k
                m = (n + 1, c + 1, 1 - b)
                dve.wait_ge(s["reads_ps"], n + 1 + CREDIT)
                tt(c_in[:, :, :], read[:, :, 0, :], R[:, b, :, 0, 0:CH], ALU.mult).then_inc(s["c_in_s"], 1)
                if left:
                    decays_a(*m)
                dve.wait_ge(s["c_in_s"], n + 1 + CREDIT)
                tt(c_lo[:, :, :], c_in[:, :, 0:4], bv[:, :, ds(c * CH, 4)], ALU.add).then_inc(sub_step, 1)
                tt(P2[:, :, :, 4], c_in[:, :, 4:8], bv[:, :, ds(c * CH + 4, 4)], ALU.add).then_inc(sub_step, 1)
                if left:
                    decays_b(*m)
                dve.wait_ge(sub_step, at(1))
                dve.wait_ge(s["inv_in"], n + 1 + CREDIT)
                tt(P1[:, :, :, :], INV[:, b, :, 0, :].rearrange("p h (t j) -> p h t j", t=4),
                   c_lo[:, :, :].unsqueeze(2).to_broadcast([P, H, 4, 4]), ALU.mult).then_inc(sub_step, 1)
                if left:
                    decays_c(*m)
                dve.wait_ge(sub_step, at(3))
                dve.wait_ge(s["o_in"], n - 1 + CREDIT)
                dve.tensor_reduce(U[:, b, :, 0:4], P1[:, :, :, :], X, ALU.add).then_inc(sub_step, 1)
                dve.wait_ge(sub_step, at(4))
                tt(P2[:, :, :, 0:4], W64[:, b, :, 4:8, 0:4], U[:, b, :, 0:4].unsqueeze(2).to_broadcast([P, H, 4, 4]),
                   ALU.mult).then_inc(sub_step, 1)
                dve.wait_ge(sub_step, at(5))
                dve.tensor_reduce(c_hi[:, :, :], P2[:, :, :, :], X, ALU.add).then_inc(sub_step, 1)
                dve.wait_ge(sub_step, at(6))
                tt(P1[:, :, :, :], INV[:, b, :, 1, :].rearrange("p h (t j) -> p h t j", t=4),
                   c_hi[:, :, :].unsqueeze(2).to_broadcast([P, H, 4, 4]), ALU.mult).then_inc(sub_step, 1)
                dve.wait_ge(sub_step, at(7))
                dve.tensor_reduce(U[:, b, :, 4:8], P1[:, :, :, :], X, ALU.add).then_inc(s["u_in"], 1)
                dve.wait_ge(s["u_in"], n + 1 + CREDIT)
                dve.wait_ge(s["ut_ps"], n + CREDIT)
                tt(uF[:, 0:H * CH].rearrange("p (h t) -> p h t", h=H), U[:, b], R[:, b, :, 1:SL, CH], ALU.mult).then_inc(s["uf_in"], 1)
                dve.wait_ge(s["dbc_ps"], n + 1 + CREDIT)
                tt(SD[:, :, :], S[:, b], dbc, ALU.mult).then_inc(s["sd_in"], 1)
                if left:
                    weights(*m)
                if left == 2:
                    products(n + 2, c + 2, b, 0, prod_k, "prodk", "gramk")
                    products(n + 2, c + 2, b, 1, prod_q, "prodq", "gramq")
                dve.wait_ge(s["upd_ps"], n + 1 + CREDIT)
                dve.wait_ge(s["sd_in"], n + 1 + CREDIT)
                tt(S[:, 1 - b], SD[:, :, :], upd, ALU.add).then_inc(s["state_in"], 1)
                if left:
                    inverses(*m)

            for name in ("prodk", "prodq", "w_in", "sd_in", "u_in", "uf_in", "state_in", "decays_in", "inv_in", "c_in_s"):
                dve.sem_inc(s[name], CREDIT)
            for x, v in ((conv_done, 2), (beta_used, 2), (gated, 2), (resid, 1), (rstd_in, 2), (routed, 1), (sd_in, 2)):
                dve.sem_inc(x, v)
            dve.wait_ge(loaded, 16 * n_loads)
            dve.wait_ge(ready_set, 9)
            with dve.Fori(0, NT) as tile:
                for f in range(16):
                    conv(tile, f)
                    if f > 4:
                        use_beta(tile, f - 1)
                use_beta(tile, 15)
                dve.drain().then_inc(tile_in, 1)
                dve.wait_ge(silu_done, tile * 16 + 16 + 2)
                dve.wait_ge(tile_in, tile + 1)
                chunk_loop(dve, tile, first, step)
                dve.wait_ge(s["o_in"], tile * NC + NC + CREDIT)

                def centre(h):
                    dve.wait_ge(mean_ps, tile * H + h + 1)
                    tt(oT[:, h, :], oT[:, h, :], bank[h % 2][:, :], ALU.subtract).then_inc(centred, 1)

                def scale_(h):
                    dve.wait_ge(sd_in, tile * H + h + 1 + 2)
                    dve.reciprocal(sd[:, h % 2, :], sd[:, h % 2, :]).then_inc(route_step, 1)
                    dve.wait_ge(route_step, tile * (H + 11) + h + 1)
                    dve.wait_ge(squared, tile * H + h + 1)
                    tt(oT[:, h, :], oT[:, h, :], sd[:, h % 2, :], ALU.mult).then_inc(rstd_in, 1)
                for h in range(H):
                    centre(h)
                    if h:
                        scale_(h - 1)
                scale_(H - 1)
                dve.drain().then_inc(normed, 1)
                for h in range(H):
                    dve.tensor_scalar(oT[:, h, :], oT[:, h, :], lnwb[:, 0:1], lnwb[:, 1:2], ALU.mult, ALU.add).then_inc(affine, 1)
                    dve.wait_ge(affine, tile * H + h + 1)
                    dve.wait_ge(gate_in, tile * H + h + 1)
                    tt(oT[:, h, :], oT[:, h, :], gt[:, h % 2, 0:TT], ALU.mult).then_inc(gated, 1)
                dve.wait_ge(xt_in, 16 * tile + 16)
                for q in range(SUB):
                    k = (tile * SUB + q) * 4
                    dve.wait_ge(y_ps, tile * SUB + q + 1 + 1)
                    tt(xt[:, q, :], xt[:, q, :], bank[6 + q % 2][:, 0:D], ALU.add).then_inc(resid, 1)
                    dve.wait_ge(resid, tile * SUB + q + 1 + 1)
                    dve.bn_stats(stat[:, 0:6], xt[:, q, :]).then_inc(ln_step, 1)
                    dve.drain()
                    dve.bn_aggr(stat[:, 6:8], stat[:, 0:6]).then_inc(ln_step, 1)
                    dve.wait_ge(ln_root, tile * SUB + q + 1)
                    dve.reciprocal(stat[:, 11:12], stat[:, 10:11]).then_inc(ln_step, 1)
                    dve.wait_ge(ln_step, k + 3)
                    stt(stat[:, 12:13], stat[:, 6:7], -1.0, stat[:, 11:12], ALU.mult, ALU.mult).then_inc(ln_step, 1)
                    dve.wait_ge(ln_step, k + 4)
                    dve.wait_ge(xT_ps, tile * SUB + q - 1 + 2)
                    dve.wait_ge(stored[q % 2], 32 * (tile * 2 + q // 2 + 1))
                    dve.tensor_scalar(x1[:, q % 2, :], xt[:, q, :], stat[:, 11:12], stat[:, 12:13], ALU.mult, ALU.add).then_inc(x1_in, 1)
                st = lambda k: tile * (H + 11) + H + k
                dve.wait_ge(logit_ps, tile * SUB + SUB + 2)
                dve.tensor_copy(L[:, :, :], bank[1][:, 0:SUB * E].rearrange("p (q e) -> p q e", q=SUB)).then_inc(route_step, 1)
                dve.wait_ge(route_step, st(1))
                dve.tensor_reduce(small[:, 0, :], L[:, :, :], X, ALU.max).then_inc(route_step, 1)
                dve.wait_ge(route_step, st(2))
                tt(L[:, :, :], L[:, :, :], small[:, 0, :].unsqueeze(2).to_broadcast([P, SUB, E]), ALU.subtract).then_inc(route_max, 1)
                dve.wait_ge(route_exp, tile + 1)
                dve.tensor_reduce(small[:, 1, :], Lp[:, :, :], X, ALU.add).then_inc(route_step, 1)
                dve.wait_ge(route_step, st(3))
                dve.reciprocal(small[:, 2, :], small[:, 1, :]).then_inc(route_step, 1)
                dve.wait_ge(route_step, st(4))
                tt(L[:, :, :], Lp[:, :, :], small[:, 2, :].unsqueeze(2).to_broadcast([P, SUB, E]), ALU.mult).then_inc(route_step, 1)
                dve.wait_ge(route_step, st(5))
                pe_, pj = (L[:, :, :].unsqueeze(u).to_broadcast([P, SUB, E, E]) for u in (3, 2))
                tt(big[:, :, :, :], pj, pe_, ALU.is_equal).then_inc(route_step, 1)
                tt(big2[:, :, :, :], pj, pe_, ALU.is_gt).then_inc(route_step, 1)
                dve.wait_ge(route_step, st(6))
                tt(big[:, :, :, :], big[:, :, :, :],
                   lower[:, :].rearrange("p (e j) -> p e j", e=E).unsqueeze(1).to_broadcast([P, SUB, E, E]),
                   ALU.mult).then_inc(route_step, 1)
                dve.wait_ge(route_step, st(8))
                tt(big[:, :, :, :], big[:, :, :, :], big2[:, :, :, :], ALU.add).then_inc(route_step, 1)
                dve.wait_ge(route_step, st(9))
                dve.tensor_reduce(Lp[:, :, :], big[:, :, :, :], X, ALU.add).then_inc(route_step, 1)
                dve.wait_ge(route_step, st(10))
                dve.tensor_scalar(Lp[:, :, :], Lp[:, :, :], 1.5, 0.5, ALU.is_lt, ALU.mult).then_inc(route_step, 1)
                dve.wait_ge(route_step, st(11))
                tt(gates_all[:, ds(tile * SUB, SUB), 0:E], L[:, :, :], Lp[:, :, :], ALU.mult).then_inc(routed, 1)


def experts(nc, io, dram, gates_all, out):
    ctx = ExitStack()
    with ctx:
        def sb(name, shape):
            return ctx.enter_context(nc.sbuf_tensor(name, shape, F32))

        def sem(name):
            return ctx.enter_context(nc.semaphore(name))

        x1T = sb("e_x1T", [P, DC, T])
        acc = sb("e_acc", [P, T // P, D])
        w1 = [sb(f"e_w1_{i}", [P, DC, FF]) for i in range(2)]
        w3 = [sb(f"e_w3_{i}", [P, DC, FF]) for i in range(2)]
        w2 = [sb(f"e_w2_{i}", [P, FB, D]) for i in range(2)]
        hT = sb("e_hT", [P, FB, TT])
        g = sb("e_g", [P, 2, TT])
        eps = sb("e_eps", [P, 1])
        st = sb("e_st", [P, 2, 16])
        y = sb("e_y", [P, 2, D])
        up1 = [ctx.enter_context(nc.psum_tensor(f"up1_{i}", [P, TT], F32)) for i in range(2)]
        up3 = [ctx.enter_context(nc.psum_tensor(f"up3_{i}", [P, TT], F32)) for i in range(2)]
        dn = [ctx.enter_context(nc.psum_tensor(f"dn_{i}", [P, TT], F32)) for i in range(SUB)]

        x_in, w_in, set_in = sem("e_x_in"), [sem(f"e_w_in{i}") for i in range(2)], sem("e_set")
        gate_ps, up_ps, gate_in, h_in = sem("e_gate_ps"), sem("e_up_ps"), sem("e_gate_in"), sem("e_h_in")
        down_ps, added = sem("e_down_ps"), sem("e_added")
        ln_step, root, y_in, y_out = sem("e_ln_step"), sem("e_root"), sem("e_y_in"), [sem(f"e_y_out{i}") for i in range(2)]
        block = ctx.enter_context(nc.Block())

        def expert_loop(eng, body):
            with eng.Fori(0, E // 2) as pair:
                for i in range(2):
                    body(pair * 2 + i, i, pair)
            body(E, 0, E // 2)

        @block.sync
        def _(sp):
            sp.dma_start(x1T[:, :, :], dram["x1T"]).then_inc(x_in, 16)
            sp.dma_start(acc[:, :, :], dram["x1"]).then_inc(x_in, 16)

            def load(e, i, pair):
                sp.wait_ge(down_ps, (e + 1) * NT * SUB + 1)
                sp.dma_start(w1[i][:, :, :], io["w1"][:, ds(e, 1), :, :].rearrange("p o c f -> p (o c) f")).then_inc(w_in[i], 16)
                sp.dma_start(w3[i][:, :, :], io["w3"][:, ds(e, 1), :, :].rearrange("p o c f -> p (o c) f")).then_inc(w_in[i], 16)
                sp.dma_start(w2[i][:, :, :], io["w2"][:, ds(e, 1), :, :].rearrange("p o c f -> p (o c) f")).then_inc(w_in[i], 16)
            expert_loop(sp, load)
            for b in range(2):
                sp.sem_inc(y_out[b], 16)
            with sp.Fori(0, T // P // 2) as i:
                for b in range(2):
                    sp.wait_ge(y_in, i * 2 + b + 1)
                    sp.dma_start(out[:, ds(i * 2 + b, 1), :], y[:, b:b + 1, :]).then_inc(y_out[b], 16)
            for b in range(2):
                sp.wait_ge(y_out[b], 16 * (T // P // 2 + 1))

        @block.gpsimd
        def _(pool):
            pool.memset(eps[:, :], EPS).then_inc(set_in, 1)
            pool.memset(gates_all[:, :, E:NE], 0.5 / E).then_inc(set_in, 1)

        @block.tensor
        def _(pe):
            pe.sem_inc(down_ps, 2 * NT * SUB + 1)
            pe.wait_ge(x_in, 32)

            def body(e, i, pair):
                with pe.Fori(0, NT) as tile:
                    pe.wait_ge(w_in[i], pair * 48 + 48)
                    n = e * NT + tile
                    for f in range(FB):
                        pe.wait_ge(h_in, n * FB + f - 1 + 2)
                        for w, ps, done in ((w1[i], up1[f % 2], gate_ps), (w3[i], up3[f % 2], up_ps)):
                            for c in range(DC):
                                k = pe.matmul(ps[:, :], w[:, c, f * P:(f + 1) * P], x1T[:, c, ds(tile * TT, TT)],
                                              start=c == 0, stop=c == DC - 1)
                            k.then_inc(done, 1)
                    for q in range(SUB):
                        pe.wait_ge(added, n * SUB + q + 1)
                        if q == 0:
                            pe.wait_ge(h_in, n * FB + FB + 2)
                        for f in range(FB):
                            k = pe.matmul(dn[q][:, 0:D], hT[:, f, q * P:(q + 1) * P], w2[i][:, f, :],
                                          start=f == 0, stop=f == FB - 1)
                        k.then_inc(down_ps, 1)
            expert_loop(pe, body)

        @block.scalar
        def _(act):
            def body(e, i, pair):
                with act.Fori(0, NT) as tile:
                    n = (e * NT + tile) * FB
                    for f in range(FB):
                        act.wait_ge(gate_ps, n + f + 1)
                        act.wait_ge(h_in, n + f - 1 + 2)
                        act.activation(g[:, f % 2, :], up1[f % 2][:, :], ACT.Silu).then_inc(gate_in, 1)
            expert_loop(act, body)
            act.wait_ge(set_in, 2)
            with act.Fori(0, T // P // 2) as i:
                for b in range(2):
                    act.wait_ge(ln_step, (i * 2 + b) * 4 + 2)
                    act.activation(st[:, b, 10:11], st[:, b, 7:8], ACT.Sqrt, bias=eps[:, :]).then_inc(root, 1)

        @block.vector
        def _(dve):
            dve.sem_inc(h_in, 2)
            dve.sem_inc(added, SUB)
            dve.wait_ge(set_in, 2)
            dve.wait_ge(x_in, 32)

            def body(e, i, pair):
                with dve.Fori(0, NT) as tile:
                    n = e * NT + tile
                    for f in range(FB):
                        dve.wait_ge(up_ps, n * FB + f + 1)
                        dve.wait_ge(gate_in, n * FB + f + 1)
                        if f == 0:
                            dve.wait_ge(down_ps, n * SUB + 2 * NT * SUB + 1)
                        dve.tensor_tensor(hT[:, f, :], g[:, f % 2, :], up3[f % 2][:, :], ALU.mult).then_inc(h_in, 1)
                    for q in range(SUB):
                        dve.wait_ge(down_ps, n * SUB + q + 1 + 2 * NT * SUB + 1)
                        dve.wait_ge(added, n * SUB + q + 1)
                        r = ds(tile * SUB + q, 1)
                        dve.scalar_tensor_tensor(acc[:, r, :].rearrange("p o d -> p (o d)"), dn[q][:, 0:D],
                                                 gates_all[:, r, ds(e, 1)].rearrange("p o d -> p (o d)"),
                                                 acc[:, r, :].rearrange("p o d -> p (o d)"), ALU.mult, ALU.add).then_inc(added, 1)
            expert_loop(dve, body)
            dve.wait_ge(added, NE * NT * SUB + SUB)
            with dve.Fori(0, T // P // 2) as i:
                for b in range(2):
                    k = (i * 2 + b) * 4
                    row = acc[:, ds(i * 2 + b, 1), :].rearrange("p o d -> p (o d)")
                    s = st[:, b, :]
                    dve.bn_stats(s[:, 0:6], row).then_inc(ln_step, 1)
                    dve.drain()
                    dve.bn_aggr(s[:, 6:8], s[:, 0:6]).then_inc(ln_step, 1)
                    dve.wait_ge(root, i * 2 + b + 1)
                    dve.reciprocal(s[:, 11:12], s[:, 10:11]).then_inc(ln_step, 1)
                    dve.wait_ge(ln_step, k + 3)
                    dve.scalar_tensor_tensor(s[:, 12:13], s[:, 6:7], -1.0, s[:, 11:12], ALU.mult, ALU.mult).then_inc(ln_step, 1)
                    dve.wait_ge(ln_step, k + 4)
                    dve.wait_ge(y_out[b], 16 * i + 16)
                    dve.tensor_scalar(y[:, b, :], row, s[:, 11:12], s[:, 12:13], ALU.mult, ALU.add).then_inc(y_in, 1)


def build(nc, io, dram, out):
    gates = nc.alloc_sbuf_tensor("gates", [P, T // P, NE], F32)
    attention(nc, io, dram, gates)
    experts(nc, io, dram, gates, out)


def kernel(**inputs):
    import numpy as _np
    import concourse.bacc as _bacc
    from concourse.bass_utils import run_bass_kernel_spmd as _run

    v = {k.split("_", 2)[2] if not k.startswith("L0_ffn") else k[len("L0_ffn_"):]: _np.asarray(x)
         for k, x in inputs.items()}

    def rows(m):
        return m.reshape(-1, P, m.shape[1]).transpose(1, 0, 2)

    perm = _np.concatenate([_np.arange(h * DK, h * DK + DK) for p in range(PR) for h in (p, p + PR)])
    x = v["x"][0]
    conv = _np.concatenate([
        _np.concatenate([v[n + "_w"][:, 0, :], v[n + "_b"][:, None]], 1)[o] for n, o in
        (("qc", perm), ("kc", perm), ("vc", _np.arange(H * DV)))])
    sel_v = _np.zeros((H, H, P), _np.float32)
    sel_p = _np.zeros((H, PR, P), _np.float32)
    for h in range(H):
        sel_v[h, h] = 1.0
        sel_p[h, h % PR, 64 * (h // PR):64 * (h // PR) + 64] = 1.0
    half_ones = _np.zeros((P, 2, P), _np.float32)
    half_ones[:DK, 0] = half_ones[DK:, 1] = 1.0
    arrays = dict(
        xT=rows(x.T), x=x.reshape(-1, P, D).transpose(1, 0, 2),
        wq=rows(v["Wq"].T[:, perm]), wk=rows(v["Wk"].T[:, perm]), wv=rows(v["Wv"].T), wa=rows(v["Wa"].T),
        wg=rows(v["Wg"].T), wo=rows(v["Wo"].T), wb=rows(v["Wb"].T), gw=rows(v["gate_W"].T),
        taps=conv.reshape(16, P, KC + 1).transpose(1, 0, 2), ba=v["ba"].reshape(H, P).T, bb=v["bb"][:, None],
        lnwb=_np.stack([v["ln_w"], v["ln_b"]], 1),
        ident=_np.eye(P, dtype=_np.float32), half_ones=half_ones,
        mean_w=_np.full((P, P), 1.0 / P, _np.float32), sel_v=sel_v, sel_p=sel_p,
        lower=_np.broadcast_to(_np.tril(_np.ones((E, E), _np.float32), -1).reshape(1, -1), (P, E * E)),
        eps=_np.full((P, 1), EPS, _np.float32),
        w1=_np.concatenate([v["w1_e"], v["w1_s"].transpose(1, 0, 2).reshape(1, D, FF)]).reshape(NE, DC, P, FF).transpose(2, 0, 1, 3),
        w3=_np.concatenate([v["w3_e"], v["w3_s"].transpose(1, 0, 2).reshape(1, D, FF)]).reshape(NE, DC, P, FF).transpose(2, 0, 1, 3),
        w2=_np.concatenate([v["w2_e"], v["w2_s"].reshape(1, FF, D)]).reshape(NE, FB, P, D).transpose(2, 0, 1, 3),
    )
    nc = _bacc.Bacc("TRN2", target_bir_lowering=False, num_devices=1)
    feeds, io = {}, {}
    for name, arr in arrays.items():
        arr = _np.ascontiguousarray(arr)
        feeds["in_" + name] = arr
        io[name] = nc.dram_tensor("in_" + name, arr.shape, mybir.dt.from_np(arr.dtype), kind="ExternalInput").ap()
    io["const_loads"] = [n for n in arrays if n not in ("x", "xT", "w1", "w3", "w2")]
    out = nc.dram_tensor("out0", (P, T // P, D), F32, kind="ExternalOutput").ap()
    dram = dict(x1=nc.dram_tensor("x1_d", (P, T // P, D), F32, kind="Internal").ap(),
                x1T=nc.dram_tensor("x1T_d", (P, DC, T), F32, kind="Internal").ap())
    build(nc, io, dram, out)
    got = _run(nc, [feeds], core_ids=[0]).results[0]["out0"]
    return got.transpose(1, 0, 2).reshape(1, T, D)
```

```python
from contextlib import ExitStack

import numpy as np
import concourse.bass as bass
from concourse import mybir

F32 = mybir.dt.float32
F32R = mybir.dt.float32r
ALU = mybir.AluOpType
ACT = mybir.ActivationFunctionType
X = mybir.AxisListType.X
ds = bass.ds

T, D = 4096, 256
H, DK, DV, KC = 8, 64, 128, 4
PR = H // 2
P = 128
DC = D // P
TT = 512
NT = T // TT
CH = 8
NC = TT // CH
SL = CH + 1
E, FF = 8, 1024
NE = E + 1
FB = FF // P
SUB = TT // P
TH, HT = T // 2, NT // 2
RH = TH // P
EPS = 1e-5
SCALE = float(DK) ** -0.5
NF = 8 + 4 + 4 + 8
CREDIT = 2


def attention(nc, io, dram, gates_all):
    ctx = ExitStack()
    with ctx:
        def sb(name, shape):
            return ctx.enter_context(nc.sbuf_tensor(name, shape, F32))

        def sem(name):
            return ctx.enter_context(nc.semaphore(name))

        wq, wk = sb("wq", [P, DC, H * DK]), sb("wk", [P, DC, H * DK])
        wv, wa, wg = (sb(n, [P, DC, H * DV]) for n in ("wv", "wa", "wg"))
        wo = sb("wo", [P, H, D])
        wb = sb("wb", [P, DC, H])
        gw = sb("gw", [P, DC, E])
        taps = sb("taps", [P, 16, KC + 1])
        ba = sb("ba", [P, H])
        bb = sb("bb", [H, 1])
        lnwb = sb("lnwb", [P, 2])
        ident, mean_w = (sb(n, [P, P]) for n in ("ident", "mean_w"))
        half_ones = sb("half_ones", [P, 2, P])
        sel_v = sb("sel_v", [H, H, P])
        sel_p = sb("sel_p", [H, PR, P])
        lower = sb("lower", [P, E * E])
        eps = sb("eps", [P, 1])
        xT = sb("xT", [P, DC, TT])
        xt = sb("xt", [P, SUB, D])
        a = sb("a", [P, H, TT])
        bv = sb("bv", [P, H, TT])
        K = sb("K", [P, PR, TT])
        QK = sb("QK", [P, PR, 2, TT])
        oT = sb("oT", [P, H, TT])
        halo = sb("halo", [P, 16, KC - 1])
        raw = sb("raw", [P, 2, KC - 1 + TT])
        acc = sb("acc", [P, 2, TT])
        sil = sb("sil", [P, 2, TT])
        beta = sb("beta", [H, TT])
        R = sb("R", [P, 2, H, SL, SL])
        W = sb("W", [P, 2, H, 72])
        INV = sb("INV", [P, 2, H, 2, 16])
        inv_tmp = sb("inv_tmp", [P, H, 2, 3])
        prod_k = sb("prod_k", [P, PR, CH, CH])
        prod_q = sb("prod_q", [P, PR, CH, CH])
        kexp = sb("kexp", [P, H * CH])
        own_pair = sb("own_pair", [H * CH, PR])
        qkx = sb("qkx", [P, 2, PR, 2, 2, CH])
        Krow = sb("Krow", [H * CH, 2, PR, P])
        gq = sb("gq", [P, H, CH, CH])
        Nq = sb("Nq", [P, 2, H, CH, CH])
        rq = sb("rq", [P, H, CH])
        tree = sb("tree", [P, H, CH, 8])
        rsc = sb("rsc", [P, H, CH])
        c_in = sb("c_in", [P, H, CH])
        c_lo = sb("c_lo", [P, H, 4])
        P1 = sb("P1", [P, H, 4, 4])
        P2 = sb("P2", [P, H, 4, 5])
        c_hi = sb("c_hi", [P, H, 4])
        U = sb("U", [P, 2, H, CH])
        uF = sb("uF", [P, P])
        uT = sb("uT", [H * CH, P])
        dT = sb("dT", [H, P])
        S = sb("S", [P, 2, PR, P])
        SD = sb("SD", [P, PR, P])
        sq = acc
        sd = sil
        gt = raw
        x1 = sb("x1", [P, 2, D])
        x1T = sb("x1T", [P, 2, DC, P])
        stat = sb("stat", [P, 16])
        L = sb("L", [P, SUB, E])
        big = sb("big", [P, SUB, E, E])
        big2 = sb("big2", [P, SUB, E, E])
        small = sb("small", [P, 4, SUB])
        Lp = sb("Lp", [P, SUB, E])

        bank = [ctx.enter_context(nc.psum_tensor(f"bank{i}", [P, 512], F32)) for i in range(8)]
        g_k = bank[0][:, :].rearrange("p (h t j) -> p h t j", h=H, t=CH)
        g_q = bank[1][:, :].rearrange("p (h t j) -> p h t j", h=H, t=CH)
        k_row = bank[2][0:H * CH, 0:P]
        upd = bank[3][:, :].rearrange("p (r v) -> p r v", r=PR)
        dbc = bank[4][:, :].rearrange("p (r v) -> p r v", r=PR)
        read = bank[5][:, 0:128].rearrange("p (h x t) -> p h x t", h=H, x=2)
        read_p = bank[5][:, 0:128].rearrange("p (g r y) -> p r g y", g=2, r=PR)
        u_row = bank[6][:, 0:P]
        d_row = bank[7][0:H, 0:P]

        R81 = R[:, :, :, :, :].rearrange("p b h s r -> p b h (s r)")
        W64 = W[:, :, :, 0:64].rearrange("p b h (t j) -> p b h t j", t=CH)
        W36 = W[:, :, :, :].rearrange("p b h (k r) -> p b h k r", k=2)

        loaded = sem("loaded")
        ready_set = sem("ready_set")
        xT_in = sem("xT_in")
        xt_in = sem("xt_in")
        stored = [sem(f"stored{i}") for i in range(2)]
        beta_logit = sem("beta_logit")
        beta_sig = sem("beta_sig")
        projected = sem("projected")
        evacuated = sem("evacuated")
        raw_in = sem("raw_in")
        tap = sem("tap")
        halo_in = sem("halo_in")
        conv_done = sem("conv_done")
        silu_done = sem("silu_done")
        beta_bc = sem("beta_bc")
        beta_used = sem("beta_used")
        key_step = sem("key_step")
        tile_in = sem("tile_in")
        names = ("slots_in", "rq_in", "qkx_in", "kexp_in", "krow_in", "gq_in", "ut_in", "dt_in",
                 "slots_used", "prodk", "prodq", "w_in", "sd_in", "u_in", "uf_in", "state_in", "cin_used",
                 "gramk", "gramq", "krow_ps", "reads_ps", "ut_ps", "dt_ps", "dbc_ps", "upd_ps",
                 "nq_in", "o_in", "rs_in", "decays_in", "inv_in", "c_in_s")
        s = {n: sem("s_" + n) for n in names}
        decay_step = sem("decay_step")
        inv_step = sem("inv_step")
        sub_step = sem("sub_step")
        out_step = sem("out_step")
        mean_ps, centred, squared, var_ps, sd_in, normed = (sem(n) for n in (
            "mean_ps", "centred", "squared", "var_ps", "sd_root", "normed"))
        rstd_in = sem("rstd_in")
        gate_ps, gate_in, affine, gated = (sem(n) for n in ("gate_ps", "gate_in", "affine", "gated"))
        y_ps, resid, ln_step, ln_root, x1_in = (sem(n) for n in ("y_ps", "resid", "ln_step", "ln_root", "x1_in"))
        xT_ps, x1T_in, logit_ps = (sem(n) for n in ("xT_ps", "x1T_in", "logit_ps"))
        route_step, route_max, route_exp, routed = (sem(n) for n in ("route_step", "route_max", "route_exp", "routed"))

        block = ctx.enter_context(nc.Block())
        n_loads = len(io["const_loads"])
        consts = dict(wq=wq, wk=wk, wv=wv, wa=wa, wg=wg, wo=wo, wb=wb, gw=gw, taps=taps, ba=ba, bb=bb,
                      lnwb=lnwb, ident=ident, own_pair=own_pair, half_ones=half_ones, mean_w=mean_w, sel_v=sel_v, sel_p=sel_p,
                      lower=lower, eps=eps)

        def chunk_loop(eng, tile, first, step):
            first(tile * NC, 0, 0)
            with eng.Fori(0, NC // 2 - 1) as i:
                for b in range(2):
                    step(tile * NC + i * 2 + b, i * 2 + b, b, 2)
            step(tile * NC + NC - 2, NC - 2, 0, 1)
            step(tile * NC + NC - 1, NC - 1, 1, 0)

        @block.sync
        def _(sp):
            for name in io["const_loads"]:
                t = consts[name]
                sp.dma_start(t.ap(), io[name]).then_inc(loaded, 16)
            for b in range(2):
                sp.sem_inc(stored[b], 32)
            with sp.Fori(0, NT) as tile:
                sp.wait_ge(gate_ps, tile * H + 1)
                sp.dma_start(xT[:, :, :], io["xT"][:, :, ds(tile * TT, TT)]).then_inc(xT_in, 16)
                sp.dma_start(xt[:, :, :], io["x"][:, ds(tile * SUB, SUB), :]).then_inc(xt_in, 16)
                for q in range(SUB):
                    sp.wait_ge(x1_in, tile * SUB + q + 1)
                    sp.dma_start(dram["x1"][:, ds(tile * SUB + q, 1), :], x1[:, q % 2:q % 2 + 1, :]).then_inc(stored[q % 2], 16)
                    sp.wait_ge(x1T_in, tile * SUB + q + 1)
                    sp.dma_start(dram["x1T"][:, :, ds(tile * TT + q * P, P)], x1T[:, q % 2, :, :]).then_inc(stored[q % 2], 16)
            for b in range(2):
                sp.wait_ge(stored[b], 32 * (NT * SUB // 2 + 1))

        @block.gpsimd
        def _(pool):
            for t in (kexp[:, :], qkx[:, :, :, :, :, :], halo[:, :, :], S[:, :, :, :], INV[:, :, :, :, :], uF[:, :]):
                pool.memset(t, 0.0).then_inc(ready_set, 1)
            pool.memset(R81[:, :, :, :], 0.0).then_inc(ready_set, 1)
            pool.wait_ge(ready_set, 7)
            pool.memset(R81[:, :, :, 0:81:10], 1.0).then_inc(ready_set, 1)
            pool.memset(INV[:, :, :, :, 0:16:5], 1.0).then_inc(ready_set, 1)
            pool.wait_ge(ready_set, 9)

            def weigh(n, c, b):
                pool.wait_ge(s["gq_in"], n + 1 + CREDIT)
                pool.wait_ge(s["decays_in"], n + 1 + CREDIT)
                pool.tensor_tensor(Nq[:, b], gq[:, :, :, :],
                                   R[:, b, :, 1:SL, 1:SL].rearrange("p h j t -> p h t j"), ALU.mult)\
                    .then_inc(s["nq_in"], 1)

            def outputs(n, c, b):
                pool.wait_ge(s["rq_in"], n + 1 + CREDIT)
                pool.wait_ge(s["o_in"], n + CREDIT)
                pool.tensor_tensor(rsc[:, :, :], rq[:, :, :], R[:, b, :, 0, 1:SL], ALU.mult).then_inc(s["rs_in"], 1)
                pool.wait_ge(s["u_in"], n + 1 + CREDIT)
                pool.wait_ge(s["nq_in"], n + 1 + CREDIT)
                pool.tensor_tensor(Nq[:, b], Nq[:, b],
                                   U[:, b].unsqueeze(2).to_broadcast([P, H, CH, CH]), ALU.mult).then_inc(out_step, 1)
                pool.wait_ge(out_step, n * 4 + 1 + CREDIT * 4)
                pool.tensor_tensor(tree[:, :, :, 0:4], Nq[:, b, :, :, 0:4], Nq[:, b, :, :, 4:8], ALU.add).then_inc(out_step, 1)
                pool.wait_ge(out_step, n * 4 + 2 + CREDIT * 4)
                pool.tensor_tensor(tree[:, :, :, 4:6], tree[:, :, :, 0:2], tree[:, :, :, 2:4], ALU.add).then_inc(out_step, 1)
                pool.wait_ge(out_step, n * 4 + 3 + CREDIT * 4)
                pool.wait_ge(s["rs_in"], n + 1 + CREDIT)
                pool.tensor_tensor(tree[:, :, :, 6], tree[:, :, :, 4], tree[:, :, :, 5], ALU.add).then_inc(out_step, 1)
                pool.wait_ge(out_step, n * 4 + 4 + CREDIT * 4)
                pool.tensor_tensor(oT[:, :, ds(c * CH, CH)], tree[:, :, :, 6], rsc[:, :, :], ALU.add).then_inc(s["o_in"], 1)

            def step(n, c, b, left):
                outputs(n, c, b)
                if left:
                    weigh(n + 1, c + 1, 1 - b)

            pool.sem_inc(out_step, 4 * CREDIT)
            for name in ("nq_in", "rs_in", "o_in"):
                pool.sem_inc(s[name], CREDIT)
            with pool.Fori(0, NT) as tile:
                pool.wait_ge(gated, tile * H + 2)
                pool.wait_ge(y_ps, tile * SUB + 1)
                chunk_loop(pool, tile, weigh, step)

        @block.scalar
        def _(act):
            def conv_part(tile, f):
                e = 8 + f
                act.wait_ge(projected, tile * NF + e + 1)
                act.wait_ge(conv_done, tile * 16 + f - 1 + 2)
                act.wait_ge(silu_done, tile * 16 + f - 1 + 2)
                act.copy(raw[:, f % 2, KC - 1:], bank[e % 2][:, :]).then_inc(raw_in, 1)
                act.activation(acc[:, f % 2, :], bank[e % 2][:, :], ACT.Identity, bias=taps[:, f, KC:KC + 1],
                               scale=taps[:, f, KC - 1:KC]).then_inc(evacuated, 1)

            def silu_part(tile, f):
                act.wait_ge(conv_done, tile * 16 + f + 1 + 2)
                if f >= 4:
                    act.wait_ge(beta_used, tile * 12 + f - 4 - 1 + 2)
                dst = QK[:, f, 1, :] if f < 4 else sil[:, f % 2, :]
                act.activation(dst, acc[:, f % 2, :], ACT.Silu).then_inc(silu_done, 1)

            def prepare(n, c, b):
                act.wait_ge(s["uf_in"], n - 1 + CREDIT)
                act.wait_ge(s["dt_ps"], n - 1 + CREDIT)
                act.wait_ge(s["rs_in"], n - 1 + CREDIT)
                act.wait_ge(s["w_in"], n - 1 + CREDIT)
                act.copy(R81[:, b, :, 1:72:10], a[:, :, ds(c * CH, CH)]).then_inc(s["slots_in"], 1)

            def stage(n, c, b):
                act.wait_ge(s["reads_ps"], n - 1 + CREDIT)
                for half in range(2):
                    r = slice(64 * half, 64 * half + 64)
                    i = act.copy(qkx[r, b, :, half, :, :], QK[r, :, :, ds(c * CH, CH)])
                i.then_inc(s["qkx_in"], 1)
                act.wait_ge(s["krow_ps"], n + CREDIT)
                for half in range(2):
                    r = slice(64 * half, 64 * half + 64)
                    i = act.copy(kexp[r, 32 * half:32 * half + 32].rearrange("p (r t) -> p r t", r=PR), K[r, :, ds(c * CH, CH)])
                i.then_inc(s["kexp_in"], 1)

            def finish(n, c, b):
                act.wait_ge(s["dt_ps"], n + 1 + CREDIT)
                act.wait_ge(s["dbc_ps"], n + CREDIT)
                act.copy(dT[:, :], d_row).then_inc(s["dt_in"], 1)
                act.wait_ge(s["krow_ps"], n + 1 + CREDIT)
                act.wait_ge(s["upd_ps"], n - 1 + CREDIT)
                for p in range(PR):
                    i = act.activation(Krow[:, b, p, :], k_row, ACT.Identity, scale=own_pair[:, p:p + 1])
                i.then_inc(s["krow_in"], 1)
                act.wait_ge(s["gramq"], n + 1 + CREDIT)
                act.wait_ge(s["nq_in"], n + CREDIT)
                act.copy(gq[:, :, :, :], g_q).then_inc(s["gq_in"], 1)

            def first(n, c, b):
                prepare(n, c, b)
                stage(n, c, b)
                finish(n, c, b)
                prepare(n + 1, c + 1, 1 - b)

            def step(n, c, b, left):
                act.wait_ge(s["c_in_s"], n + 1 + CREDIT)
                act.wait_ge(s["rs_in"], n + CREDIT)
                act.copy(rq[:, :, :], read[:, :, 1, :]).then_inc(s["rq_in"], 1)
                if left:
                    stage(n + 1, c + 1, 1 - b)
                act.wait_ge(s["ut_ps"], n + 1 + CREDIT)
                act.wait_ge(s["upd_ps"], n + CREDIT)
                act.copy(uT[:, :], u_row[0:H * CH, :]).then_inc(s["ut_in"], 1)
                if left:
                    finish(n + 1, c + 1, 1 - b)
                if left == 2:
                    prepare(n + 2, c + 2, b)

            act.wait_ge(loaded, 16 * n_loads)
            act.wait_ge(ready_set, 9)
            for name in ("slots_in", "rq_in", "qkx_in", "kexp_in", "krow_in", "gq_in", "ut_in", "dt_in"):
                act.sem_inc(s[name], CREDIT)
            act.sem_inc(silu_done, 2)
            with act.Fori(0, NT) as tile:
                act.wait_ge(beta_logit, tile + 1)
                act.activation(beta[:, :], bank[4][0:H, :], ACT.Sigmoid, bias=bb[:, :]).then_inc(beta_sig, 1)
                for e in range(H):
                    act.wait_ge(projected, tile * NF + e + 1)
                    act.activation(a[:, e, :], bank[e % 2][:, :], ACT.Sigmoid, bias=ba[:, e:e + 1]).then_inc(evacuated, 1)
                for f in range(16):
                    conv_part(tile, f)
                    if f:
                        silu_part(tile, f - 1)
                silu_part(tile, 15)
                act.wait_ge(tile_in, tile + 1)
                act.wait_ge(silu_done, tile * 16 + 16 + 2)
                chunk_loop(act, tile, first, step)
                for h in range(H):
                    act.wait_ge(centred, tile * H + h + 1)
                    act.wait_ge(var_ps, tile * H + h - 1 + 2)
                    act.activation(sq[:, h % 2, :], oT[:, h, :], ACT.Square).then_inc(squared, 1)
                    act.wait_ge(var_ps, tile * H + h + 1 + 2)
                    act.wait_ge(rstd_in, tile * H + h - 1 + 2)
                    act.activation(sd[:, h % 2, :], bank[2 + h % 2][:, :], ACT.Sqrt, bias=eps[:, :]).then_inc(sd_in, 1)
                for h in range(H):
                    act.wait_ge(gate_ps, tile * H + h + 1 + 1)
                    act.wait_ge(gated, tile * H + h - 1 + 2)
                    act.activation(gt[:, h % 2, 0:TT], bank[4 + h % 2][:, :], ACT.Sigmoid).then_inc(gate_in, 1)
                for q in range(SUB):
                    act.wait_ge(ln_step, (tile * SUB + q) * 4 + 2)
                    act.activation(stat[:, 10:11], stat[:, 7:8], ACT.Sqrt, bias=eps[:, :]).then_inc(ln_root, 1)
                    act.wait_ge(xT_ps, tile * SUB + q + 1 + 2)
                    act.wait_ge(stored[q % 2], 32 * (tile * 2 + q // 2 + 1))
                    act.wait_ge(logit_ps, tile * SUB + q - 1 + 2)
                    act.copy(x1T[:, q % 2], bank[0][:, 0:D].rearrange("p (c t) -> p c t", c=DC)).then_inc(x1T_in, 1)
                act.wait_ge(route_max, tile + 1)
                act.activation(Lp[:, :, :], L[:, :, :], ACT.Exp).then_inc(route_exp, 1)

        @block.tensor
        def _(pe):
            mm, tr = pe.matmul, pe.transpose

            def project(out, w, e):
                for c in range(DC):
                    i = mm(out, w[:, c, e * P:(e + 1) * P], xT[:, c, :], start=c == 0, stop=c == DC - 1)
                return i

            def grams(n, c, b):
                for ps, prod, made, done, used in ((g_k, prod_k, "prodk", "gramk", "w_in"),
                                                  (g_q, prod_q, "prodq", "gramq", "gq_in")):
                    pe.wait_ge(s[made], n + 1 + CREDIT)
                    pe.wait_ge(s[used], n + CREDIT)
                    for half in range(2):
                        i = mm(ps[:, 4 * half:4 * half + 4], half_ones[:, half, :], prod[:, :, :, :], start=True, stop=True)
                    i.then_inc(s[done], 1)

            def key_rows(n, c, b):
                tr(k_row, kexp[:, :], ident[:, :]).then_inc(s["krow_ps"], 1)

            def decay_row(n, c, b):
                pe.wait_ge(s["kexp_in"], n + 1 + CREDIT)
                pe.wait_ge(s["krow_in"], n + CREDIT)
                pe.wait_ge(s["decays_in"], n + 1 + CREDIT)
                pe.wait_ge(s["dt_in"], n + CREDIT)
                tr(d_row, R[:, b, :, 0, CH], ident[:, :]).then_inc(s["dt_ps"], 1)

            def decay_bc(n, c, b):
                pe.wait_ge(s["dt_in"], n + 1 + CREDIT)
                pe.wait_ge(s["sd_in"], n + CREDIT)
                for p in range(PR):
                    i = mm(dbc[:, p, :], sel_p[:, p, :], dT[:, :], start=True, stop=True)
                i.then_inc(s["dbc_ps"], 1)

            def first(n, c, b):
                grams(n, c, b)
                decay_row(n, c, b)
                key_rows(n, c, b)
                decay_bc(n, c, b)

            def step(n, c, b, left):
                pe.wait_ge(s["state_in"], n + CREDIT)
                pe.wait_ge(s["qkx_in"], n + 1 + CREDIT)
                pe.wait_ge(s["rq_in"], n + CREDIT)
                pe.wait_ge(s["c_in_s"], n + CREDIT)
                for p in range(PR):
                    i = mm(read_p[:, p], S[:, b, p, :], qkx[:, b, p].rearrange("p g x t -> p (g x t)"), start=True, stop=True)
                i.then_inc(s["reads_ps"], 1)
                if left:
                    grams(n + 1, c + 1, 1 - b)
                pe.wait_ge(s["uf_in"], n + 1 + CREDIT)
                pe.wait_ge(s["ut_in"], n + CREDIT)
                tr(u_row, uF[:, :], ident[:, :]).then_inc(s["ut_ps"], 1)
                if left:
                    decay_row(n + 1, c + 1, 1 - b)
                pe.wait_ge(s["ut_in"], n + 1 + CREDIT)
                pe.wait_ge(s["krow_in"], n + 1 + CREDIT)
                pe.wait_ge(s["state_in"], n + CREDIT)
                for p in range(PR):
                    i = mm(upd[:, p, :], Krow[:, b, p, :], uT[:, :], start=True, stop=True)
                i.then_inc(s["upd_ps"], 1)
                if left:
                    key_rows(n + 1, c + 1, 1 - b)
                    decay_bc(n + 1, c + 1, 1 - b)

            pe.wait_ge(loaded, 16 * n_loads)
            pe.wait_ge(ready_set, 9)
            for name in ("gramk", "gramq", "krow_ps", "reads_ps", "ut_ps", "dt_ps", "dbc_ps", "upd_ps"):
                pe.sem_inc(s[name], CREDIT)
            pe.sem_inc(gate_ps, 1)
            pe.sem_inc(y_ps, 1)
            pe.sem_inc(var_ps, 2)
            pe.sem_inc(xT_ps, 2)
            pe.sem_inc(logit_ps, 2)
            with pe.Fori(0, NT) as tile:
                pe.wait_ge(xT_in, 16 * tile + 16)
                pe.wait_ge(routed, tile + 1)
                for c in range(DC):
                    i = mm(bank[4][0:H, :], wb[:, c, :], xT[:, c, :], start=c == 0, stop=c == DC - 1)
                i.then_inc(beta_logit, 1)
                parts = [(wa, h) for h in range(H)] + [(wq, p) for p in range(PR)] + [(wk, p) for p in range(PR)]\
                    + [(wv, h) for h in range(H)]
                for e, (w, j) in enumerate(parts):
                    if e >= 2:
                        pe.wait_ge(evacuated, tile * NF + e - 1)
                    project(bank[e % 2][:, :], w, j).then_inc(projected, 1)
                    if e >= 12:
                        j = e - 12
                        if j == 0:
                            pe.wait_ge(beta_sig, tile + 1)
                        pe.wait_ge(beta_used, tile * 12 + j - 1 + 2)
                        sel = sel_p[:, j, :] if j < PR else sel_v[:, j - PR, :]
                        mm(bank[2 + j % 2][:, :], sel, beta[:, :], start=True, stop=True).then_inc(beta_bc, 1)
                pe.wait_ge(evacuated, tile * NF + NF)
                pe.wait_ge(tile_in, tile + 1)
                chunk_loop(pe, tile, first, step)
                pe.wait_ge(s["o_in"], tile * NC + NC + CREDIT)
                pe.wait_ge(s["state_in"], tile * NC + NC + CREDIT)

                def variance(h):
                    pe.wait_ge(squared, tile * H + h + 1)
                    pe.wait_ge(sd_in, tile * H + h - 1 + 2)
                    mm(bank[2 + h % 2][:, :], mean_w[:, :], sq[:, h % 2, :], start=True, stop=True).then_inc(var_ps, 1)
                for h in range(H):
                    if h >= 2:
                        pe.wait_ge(centred, tile * H + h - 1)
                    mm(bank[h % 2][:, :], mean_w[:, :], oT[:, h, :], start=True, stop=True).then_inc(mean_ps, 1)
                    if h:
                        variance(h - 1)
                variance(H - 1)
                for h in range(H):
                    if h >= 2:
                        pe.wait_ge(gate_in, tile * H + h - 1)
                    project(bank[4 + h % 2][:, :], wg, h).then_inc(gate_ps, 1)

                def transposes(q):
                    pe.wait_ge(x1_in, tile * SUB + q + 1)
                    if q:
                        pe.wait_ge(x1T_in, tile * SUB + q)
                    else:
                        pe.wait_ge(normed, tile + 1)
                    for c in range(DC):
                        i = tr(bank[0][:, c * P:(c + 1) * P], x1[:, q % 2, c * P:(c + 1) * P], ident[:, :])
                    i.then_inc(xT_ps, 1)

                def logits(q):
                    pe.wait_ge(x1T_in, tile * SUB + q + 1)
                    for c in range(DC):
                        i = mm(bank[1][:, q * E:(q + 1) * E], x1T[:, q % 2, c, :], gw[:, c, :], start=c == 0, stop=c == DC - 1)
                    i.then_inc(logit_ps, 1)
                pe.wait_ge(gated, tile * H + H + 2)
                for q in range(SUB):
                    if q >= 2:
                        pe.wait_ge(resid, tile * SUB + q - 1 + 1)
                    for h in range(H):
                        i = mm(bank[6 + q % 2][:, 0:D], oT[:, h, q * P:(q + 1) * P], wo[:, h, :], start=h == 0, stop=h == H - 1)
                    i.then_inc(y_ps, 1)
                for q in range(SUB):
                    transposes(q)
                    logits(q)

        @block.vector
        def _(dve):
            tt, stt = dve.tensor_tensor, dve.scalar_tensor_tensor

            def conv(tile, f):
                b = f % 2
                dve.tensor_copy(raw[:, b, 0:KC - 1], halo[:, f, :]).then_inc(halo_in, 1)
                dve.wait_ge(halo_in, tile * 16 + f + 1)
                dve.wait_ge(raw_in, tile * 16 + f + 1)
                dve.wait_ge(evacuated, tile * NF + 8 + f + 1)
                for k in range(KC - 1):
                    if k:
                        dve.wait_ge(tap, tile * 48 + 3 * f + k)
                    i = stt(acc[:, b, :], raw[:, b, k:k + TT], taps[:, f, k:k + 1], acc[:, b, :], ALU.mult, ALU.add)
                    i.then_inc(tap, 1)
                dve.wait_ge(tap, tile * 48 + 3 * f + 3)
                dve.tensor_copy(halo[:, f, :], raw[:, b, TT:]).then_inc(conv_done, 1)

            def use_beta(tile, f):
                j = f - 4
                dve.wait_ge(silu_done, tile * 16 + f + 1 + 2)
                dve.wait_ge(beta_bc, tile * 12 + j + 1)
                ps = bank[2 + j % 2][:, :]
                if j < PR:
                    dve.tensor_scalar(K[:, j, :], sil[:, f % 2, :], SCALE, None, ALU.mult).then_inc(key_step, 1)
                    stt(QK[:, j, 0, :], sil[:, f % 2, :], -SCALE, ps, ALU.mult, ALU.mult).then_inc(beta_used, 1)
                else:
                    tt(bv[:, j - PR, :], sil[:, f % 2, :], ps, ALU.mult).then_inc(beta_used, 1)

            def decays_a(n, c, b):
                dve.wait_ge(s["slots_in"], n + 1 + CREDIT)
                tt(R81[:, b, :, 2:63:20], R81[:, b, :, 1:62:20], R81[:, b, :, 11:72:20], ALU.mult).then_inc(decay_step, 1)

            def decays_b(n, c, b):
                dve.wait_ge(decay_step, n * 3 + 1)
                for o in (0, 4):
                    tt(R[:, b, :, o:o + 2, o + 3:o + 5], R[:, b, :, o:o + 2, o + 2:o + 3].to_broadcast([P, H, 2, 2]),
                       R[:, b, :, o + 2:o + 3, o + 3:o + 5].to_broadcast([P, H, 2, 2]), ALU.mult).then_inc(decay_step, 1)

            def decays_c(n, c, b):
                dve.wait_ge(decay_step, n * 3 + 3)
                tt(R[:, b, :, 0:4, 5:9], R[:, b, :, 0:4, 4:5].to_broadcast([P, H, 4, 4]),
                   R[:, b, :, 4:5, 5:9].to_broadcast([P, H, 4, 4]), ALU.mult).then_inc(s["decays_in"], 1)

            def products(n, c, b, x, out, made, used):
                dve.wait_ge(s[used], n + CREDIT)
                tok = ds(c * CH, CH)
                tt(out[:, :, :, :], QK[:, :, x, tok].unsqueeze(3).to_broadcast([P, PR, CH, CH]),
                   K[:, :, tok].unsqueeze(2).to_broadcast([P, PR, CH, CH]), ALU.mult).then_inc(s[made], 1)

            def weights(n, c, b):
                dve.wait_ge(s["gramk"], n + 1 + CREDIT)
                dve.wait_ge(s["decays_in"], n + 1 + CREDIT)
                tt(W64[:, b, :, 1:8, 0:7], g_k[:, :, 1:8, 0:7], R[:, b, :, 1:8, 1:8].rearrange("p h j t -> p h t j"),
                   ALU.mult).then_inc(s["w_in"], 1)

            def inverses(n, c, b):
                w, v, m = W36[:, b], INV[:, b], inv_tmp
                dve.wait_ge(s["w_in"], n + 1 + CREDIT)
                dve.tensor_copy(v[:, :, :, 4:15:5], w[:, :, :, 8:27:9]).then_inc(inv_step, 1)
                tt(m[:, :, :, 0:2], w[:, :, :, 17:27:9], w[:, :, :, 8:18:9], ALU.mult).then_inc(inv_step, 1)
                dve.wait_ge(inv_step, n * 5 + 2)
                tt(v[:, :, :, 8:14:5], m[:, :, :, 0:2], w[:, :, :, 16:26:9], ALU.add).then_inc(inv_step, 1)
                dve.wait_ge(inv_step, n * 5 + 3)
                tt(m[:, :, :, 0:2], w[:, :, :, 25:27], v[:, :, :, 4:9:4], ALU.mult).then_inc(inv_step, 1)
                dve.wait_ge(inv_step, n * 5 + 4)
                tt(m[:, :, :, 2], m[:, :, :, 0], m[:, :, :, 1], ALU.add).then_inc(inv_step, 1)
                dve.wait_ge(inv_step, n * 5 + 5)
                tt(v[:, :, :, 12], m[:, :, :, 2], w[:, :, :, 24], ALU.add).then_inc(s["inv_in"], 1)

            def first(n, c, b):
                decays_a(n, c, b)
                products(n, c, b, 0, prod_k, "prodk", "gramk")
                decays_b(n, c, b)
                products(n, c, b, 1, prod_q, "prodq", "gramq")
                decays_c(n, c, b)
                weights(n, c, b)
                inverses(n, c, b)
                products(n + 1, c + 1, b, 0, prod_k, "prodk", "gramk")
                products(n + 1, c + 1, b, 1, prod_q, "prodq", "gramq")

            def step(n, c, b, left):
                at = lambda k: n * 7 + k
                m = (n + 1, c + 1, 1 - b)
                dve.wait_ge(s["reads_ps"], n + 1 + CREDIT)
                tt(c_in[:, :, :], read[:, :, 0, :], R[:, b, :, 0, 0:CH], ALU.mult).then_inc(s["c_in_s"], 1)
                if left:
                    decays_a(*m)
                dve.wait_ge(s["c_in_s"], n + 1 + CREDIT)
                tt(c_lo[:, :, :], c_in[:, :, 0:4], bv[:, :, ds(c * CH, 4)], ALU.add).then_inc(sub_step, 1)
                tt(P2[:, :, :, 4], c_in[:, :, 4:8], bv[:, :, ds(c * CH + 4, 4)], ALU.add).then_inc(sub_step, 1)
                if left:
                    decays_b(*m)
                dve.wait_ge(sub_step, at(1))
                dve.wait_ge(s["inv_in"], n + 1 + CREDIT)
                tt(P1[:, :, :, :], INV[:, b, :, 0, :].rearrange("p h (t j) -> p h t j", t=4),
                   c_lo[:, :, :].unsqueeze(2).to_broadcast([P, H, 4, 4]), ALU.mult).then_inc(sub_step, 1)
                if left:
                    decays_c(*m)
                dve.wait_ge(sub_step, at(3))
                dve.wait_ge(s["o_in"], n - 1 + CREDIT)
                dve.tensor_reduce(U[:, b, :, 0:4], P1[:, :, :, :], X, ALU.add).then_inc(sub_step, 1)
                dve.wait_ge(sub_step, at(4))
                tt(P2[:, :, :, 0:4], W64[:, b, :, 4:8, 0:4], U[:, b, :, 0:4].unsqueeze(2).to_broadcast([P, H, 4, 4]),
                   ALU.mult).then_inc(sub_step, 1)
                dve.wait_ge(sub_step, at(5))
                dve.tensor_reduce(c_hi[:, :, :], P2[:, :, :, :], X, ALU.add).then_inc(sub_step, 1)
                dve.wait_ge(sub_step, at(6))
                tt(P1[:, :, :, :], INV[:, b, :, 1, :].rearrange("p h (t j) -> p h t j", t=4),
                   c_hi[:, :, :].unsqueeze(2).to_broadcast([P, H, 4, 4]), ALU.mult).then_inc(sub_step, 1)
                dve.wait_ge(sub_step, at(7))
                dve.tensor_reduce(U[:, b, :, 4:8], P1[:, :, :, :], X, ALU.add).then_inc(s["u_in"], 1)
                dve.wait_ge(s["u_in"], n + 1 + CREDIT)
                dve.wait_ge(s["ut_ps"], n + CREDIT)
                tt(uF[:, 0:H * CH].rearrange("p (h t) -> p h t", h=H), U[:, b], R[:, b, :, 1:SL, CH], ALU.mult).then_inc(s["uf_in"], 1)
                dve.wait_ge(s["dbc_ps"], n + 1 + CREDIT)
                tt(SD[:, :, :], S[:, b], dbc, ALU.mult).then_inc(s["sd_in"], 1)
                if left:
                    weights(*m)
                if left == 2:
                    products(n + 2, c + 2, b, 0, prod_k, "prodk", "gramk")
                    products(n + 2, c + 2, b, 1, prod_q, "prodq", "gramq")
                dve.wait_ge(s["upd_ps"], n + 1 + CREDIT)
                dve.wait_ge(s["sd_in"], n + 1 + CREDIT)
                tt(S[:, 1 - b], SD[:, :, :], upd, ALU.add).then_inc(s["state_in"], 1)
                if left:
                    inverses(*m)

            for name in ("prodk", "prodq", "w_in", "sd_in", "u_in", "uf_in", "state_in", "decays_in", "inv_in", "c_in_s"):
                dve.sem_inc(s[name], CREDIT)
            for x, v in ((conv_done, 2), (beta_used, 2), (gated, 2), (resid, 1), (rstd_in, 2), (routed, 1), (sd_in, 2)):
                dve.sem_inc(x, v)
            dve.wait_ge(loaded, 16 * n_loads)
            dve.wait_ge(ready_set, 9)
            with dve.Fori(0, NT) as tile:
                for f in range(16):
                    conv(tile, f)
                    if f > 4:
                        use_beta(tile, f - 1)
                use_beta(tile, 15)
                dve.drain().then_inc(tile_in, 1)
                dve.wait_ge(silu_done, tile * 16 + 16 + 2)
                dve.wait_ge(tile_in, tile + 1)
                chunk_loop(dve, tile, first, step)
                dve.wait_ge(s["o_in"], tile * NC + NC + CREDIT)

                def centre(h):
                    dve.wait_ge(mean_ps, tile * H + h + 1)
                    tt(oT[:, h, :], oT[:, h, :], bank[h % 2][:, :], ALU.subtract).then_inc(centred, 1)

                def scale_(h):
                    dve.wait_ge(sd_in, tile * H + h + 1 + 2)
                    dve.reciprocal(sd[:, h % 2, :], sd[:, h % 2, :]).then_inc(route_step, 1)
                    dve.wait_ge(route_step, tile * (H + 11) + h + 1)
                    dve.wait_ge(squared, tile * H + h + 1)
                    tt(oT[:, h, :], oT[:, h, :], sd[:, h % 2, :], ALU.mult).then_inc(rstd_in, 1)
                for h in range(H):
                    centre(h)
                    if h:
                        scale_(h - 1)
                scale_(H - 1)
                dve.drain().then_inc(normed, 1)
                for h in range(H):
                    dve.tensor_scalar(oT[:, h, :], oT[:, h, :], lnwb[:, 0:1], lnwb[:, 1:2], ALU.mult, ALU.add).then_inc(affine, 1)
                    dve.wait_ge(affine, tile * H + h + 1)
                    dve.wait_ge(gate_in, tile * H + h + 1)
                    tt(oT[:, h, :], oT[:, h, :], gt[:, h % 2, 0:TT], ALU.mult).then_inc(gated, 1)
                dve.wait_ge(xt_in, 16 * tile + 16)
                for q in range(SUB):
                    k = (tile * SUB + q) * 4
                    dve.wait_ge(y_ps, tile * SUB + q + 1 + 1)
                    tt(xt[:, q, :], xt[:, q, :], bank[6 + q % 2][:, 0:D], ALU.add).then_inc(resid, 1)
                    dve.wait_ge(resid, tile * SUB + q + 1 + 1)
                    dve.bn_stats(stat[:, 0:6], xt[:, q, :]).then_inc(ln_step, 1)
                    dve.drain()
                    dve.bn_aggr(stat[:, 6:8], stat[:, 0:6]).then_inc(ln_step, 1)
                    dve.wait_ge(ln_root, tile * SUB + q + 1)
                    dve.reciprocal(stat[:, 11:12], stat[:, 10:11]).then_inc(ln_step, 1)
                    dve.wait_ge(ln_step, k + 3)
                    stt(stat[:, 12:13], stat[:, 6:7], -1.0, stat[:, 11:12], ALU.mult, ALU.mult).then_inc(ln_step, 1)
                    dve.wait_ge(ln_step, k + 4)
                    dve.wait_ge(xT_ps, tile * SUB + q - 1 + 2)
                    dve.wait_ge(stored[q % 2], 32 * (tile * 2 + q // 2 + 1))
                    dve.tensor_scalar(x1[:, q % 2, :], xt[:, q, :], stat[:, 11:12], stat[:, 12:13], ALU.mult, ALU.add).then_inc(x1_in, 1)
                st = lambda k: tile * (H + 11) + H + k
                dve.wait_ge(logit_ps, tile * SUB + SUB + 2)
                dve.tensor_copy(L[:, :, :], bank[1][:, 0:SUB * E].rearrange("p (q e) -> p q e", q=SUB)).then_inc(route_step, 1)
                dve.wait_ge(route_step, st(1))
                dve.tensor_reduce(small[:, 0, :], L[:, :, :], X, ALU.max).then_inc(route_step, 1)
                dve.wait_ge(route_step, st(2))
                tt(L[:, :, :], L[:, :, :], small[:, 0, :].unsqueeze(2).to_broadcast([P, SUB, E]), ALU.subtract).then_inc(route_max, 1)
                dve.wait_ge(route_exp, tile + 1)
                dve.tensor_reduce(small[:, 1, :], Lp[:, :, :], X, ALU.add).then_inc(route_step, 1)
                dve.wait_ge(route_step, st(3))
                dve.reciprocal(small[:, 2, :], small[:, 1, :]).then_inc(route_step, 1)
                dve.wait_ge(route_step, st(4))
                tt(L[:, :, :], Lp[:, :, :], small[:, 2, :].unsqueeze(2).to_broadcast([P, SUB, E]), ALU.mult).then_inc(route_step, 1)
                dve.wait_ge(route_step, st(5))
                pe_, pj = (L[:, :, :].unsqueeze(u).to_broadcast([P, SUB, E, E]) for u in (3, 2))
                tt(big[:, :, :, :], pj, pe_, ALU.is_equal).then_inc(route_step, 1)
                tt(big2[:, :, :, :], pj, pe_, ALU.is_gt).then_inc(route_step, 1)
                dve.wait_ge(route_step, st(6))
                tt(big[:, :, :, :], big[:, :, :, :],
                   lower[:, :].rearrange("p (e j) -> p e j", e=E).unsqueeze(1).to_broadcast([P, SUB, E, E]),
                   ALU.mult).then_inc(route_step, 1)
                dve.wait_ge(route_step, st(8))
                tt(big[:, :, :, :], big[:, :, :, :], big2[:, :, :, :], ALU.add).then_inc(route_step, 1)
                dve.wait_ge(route_step, st(9))
                dve.tensor_reduce(Lp[:, :, :], big[:, :, :, :], X, ALU.add).then_inc(route_step, 1)
                dve.wait_ge(route_step, st(10))
                dve.tensor_scalar(Lp[:, :, :], Lp[:, :, :], 1.5, 0.5, ALU.is_lt, ALU.mult).then_inc(route_step, 1)
                dve.wait_ge(route_step, st(11))
                tt(gates_all[:, ds(tile * SUB, SUB), 0:E], L[:, :, :], Lp[:, :, :], ALU.mult).then_inc(routed, 1)


def experts(nc, io, dram, gates_all, out):
    ctx = ExitStack()
    with ctx:
        def sb(name, shape, dtype=F32):
            return ctx.enter_context(nc.sbuf_tensor(name, shape, dtype))

        def sem(name):
            return ctx.enter_context(nc.semaphore(name))

        xs = sb("e_xs", [P, 2, DC, TH], F32R)
        acc = sb("e_acc", [P, RH, D])
        w1 = [sb(f"e_w1_{i}", [P, 2, DC * FF], F32R) for i in range(2)]
        w3 = [sb(f"e_w3_{i}", [P, 2, DC * FF], F32R) for i in range(2)]
        w2 = [sb(f"e_w2_{i}", [P, 2, FB * D], F32R) for i in range(2)]
        raw = [sb(f"e_raw_{j}", [P, DC * FF]) for j in range(3)]
        g = sb("e_g", [P, 2, TT])
        hs = sb("e_hs", [P, 3, 2, TT], F32R)
        eps = sb("e_eps", [P, 1])
        one = sb("e_one", [P, 1])
        st = sb("e_st", [P, 2, 16])
        y = sb("e_y", [P, 2, D])
        up1 = [ctx.enter_context(nc.psum_tensor(f"up1_{i}", [P, TT], F32)) for i in range(2)]
        up3 = [ctx.enter_context(nc.psum_tensor(f"up3_{i}", [P, TT], F32)) for i in range(2)]
        dn = [ctx.enter_context(nc.psum_tensor(f"dn_{i}", [P, TT], F32)) for i in range(SUB)]

        raw_in = [sem(f"e_raw_in{j}") for j in range(3)]
        split = [sem(f"e_split{j}") for j in range(3)]
        x_hi, w_hi, acc_in, set_in = sem("e_x_hi"), sem("e_w_hi"), sem("e_acc_in"), sem("e_set")
        gate_ps, up_ps, gate_in, h_in = sem("e_gate_ps"), sem("e_up_ps"), sem("e_gate_in"), sem("e_h_in")
        hi_in, lo_in = sem("e_hi_in"), sem("e_lo_in")
        down_ps, added = sem("e_down_ps"), sem("e_added")
        ln_step, root, y_in, y_out = sem("e_ln_step"), sem("e_root"), sem("e_y_in"), [sem(f"e_y_out{i}") for i in range(2)]
        block = ctx.enter_context(nc.Block())

        def expert_loop(eng, body):
            body(0, 0)
            with eng.Fori(0, E // 2) as pair:
                body(pair * 2 + 1, 1)
                body(pair * 2 + 2, 0)

        @block.sync
        def _(sp):
            def load_x(half):
                for c in range(DC):
                    sp.wait_ge(split[c], half * (NE + 1) + 1)
                    sp.dma_start(raw[c][:, :], dram["x1T"][:, c, half * TH:(half + 1) * TH]).then_inc(raw_in[c], 16)

            def load_w(half):
                def load(e, i):
                    for j, w in enumerate(("w1", "w3", "w2")):
                        used = half * (NE + 1) + 1 + e if j < 2 else half * NE + e
                        sp.wait_ge(split[j], used + 1)
                        sp.dma_start(raw[j][:, :], io[w][:, ds(e, 1), :, :].rearrange("p o c f -> p (o c f)")).then_inc(raw_in[j], 16)
                return load

            def load_acc(half):
                sp.dma_start(acc[:, :, :], dram["x1"][:, half * RH:(half + 1) * RH, :]).then_inc(acc_in, 16)

            def store_y(half):
                with sp.Fori(0, RH // 2) as i:
                    for b in range(2):
                        sp.wait_ge(y_in, i * 2 + (half * RH + b + 1))
                        sp.dma_start(out[:, ds(i * 2 + (half * RH + b), 1), :], y[:, b:b + 1, :]).then_inc(y_out[b], 16)
            for b in range(2):
                sp.sem_inc(y_out[b], 16)
            load_x(0)
            load_acc(0)
            expert_loop(sp, load_w(0))
            load_x(1)
            store_y(0)
            load_acc(1)
            expert_loop(sp, load_w(1))
            store_y(1)
            for b in range(2):
                sp.wait_ge(y_out[b], 16 * (RH + 1))

        @block.gpsimd
        def _(pool):
            pool.memset(eps[:, :], EPS).then_inc(set_in, 1)
            pool.memset(gates_all[:, :, E:NE], 0.5 / E).then_inc(set_in, 1)
            pool.memset(one[:, :], 1.0).then_inc(set_in, 1)
            pool.wait_ge(set_in, 3)
            for j in range(3):
                pool.sem_inc(split[j], 1)
            with pool.Fori(0, 2) as half:
                def split_w(e, i):
                    m = half * NE + e
                    for j, w in enumerate((w1, w3, w2)):
                        loads = half * (NE + 1) + 1 + e if j < 2 else m
                        pool.wait_ge(raw_in[j], (loads + 1) * 16)
                        pool.wait_ge(down_ps, (m if isinstance(e, int) else m - 1) * (HT * FB) + 1)
                        pool.tensor_tensor(w[i][:, 0, :], raw[j][:, :], one[:, :].to_broadcast([P, DC * FF]), ALU.mult).then_inc(w_hi, 1)
                        pool.wait_ge(w_hi, m * 3 + j + 1)
                        pool.tensor_tensor(w[i][:, 1, :], raw[j][:, :], w[i][:, 0, :].bitcast(F32), ALU.subtract).then_inc(split[j], 1)
                expert_loop(pool, split_w)

        @block.tensor
        def _(pe):
            pe.sem_inc(down_ps, 1)
            with pe.Fori(0, 2) as half:
                def body(e, i):
                    with pe.Fori(0, HT) as tile:
                        n = (half * NE + e) * HT + tile
                        x_hi_t, x_lo_t = ([xs[:, part, c, ds(tile * TT, TT)] for c in range(DC)] for part in range(2))

                        def up(f):
                            pe.wait_ge(h_in, n * FB + f - 1 + 2)
                            for w, ps, done in ((w1[i], up1[f % 2], gate_ps), (w3[i], up3[f % 2], up_ps)):
                                for c in range(DC):
                                    cols = slice(c * FF + f * P, c * FF + f * P + P)
                                    pe.matmul(ps[:, :], w[:, 0, cols], x_hi_t[c], start=c == 0, stop=False)
                                    pe.matmul(ps[:, :], w[:, 0, cols], x_lo_t[c], start=False, stop=False)
                                    k = pe.matmul(ps[:, :], w[:, 1, cols], x_hi_t[c], start=False, stop=c == DC - 1)
                                k.then_inc(done, 1)

                        def down(f):
                            pe.wait_ge(lo_in, n * FB + f + 1 + 2)
                            for q in range(SUB):
                                if f == 0:
                                    pe.wait_ge(added, n * SUB + q + 1)
                                tok, cols = slice(q * P, (q + 1) * P), slice(f * D, (f + 1) * D)
                                h_hi, h_lo = hs[:, f % 3, 0, tok], hs[:, f % 3, 1, tok]
                                pe.matmul(dn[q][:, 0:D], h_hi, w2[i][:, 0, cols], start=f == 0, stop=False)
                                pe.matmul(dn[q][:, 0:D], h_hi, w2[i][:, 1, cols], start=False, stop=False)
                                k = pe.matmul(dn[q][:, 0:D], h_lo, w2[i][:, 0, cols], start=False, stop=f == FB - 1)
                            k.then_inc(down_ps, 1)
                        pe.wait_ge(split[0], half * (NE + 1) + e + 3)
                        pe.wait_ge(split[1], half * (NE + 1) + e + 3)
                        pe.wait_ge(split[2], half * NE + e + 2)
                        for f in range(FB):
                            up(f)
                            if f >= 2:
                                down(f - 2)
                        down(FB - 2)
                        down(FB - 1)
                expert_loop(pe, body)

        @block.scalar
        def _(act):
            act.wait_ge(set_in, 3)
            with act.Fori(0, 2) as half:
                for c in range(DC):
                    act.wait_ge(raw_in[c], (half * (NE + 1) + 1) * 16)
                    act.wait_ge(down_ps, half * (NE * HT * FB) + 1)
                    act.copy(xs[:, 0, c, :], raw[c][:, :]).then_inc(x_hi, 1)

                def body(e, i):
                    with act.Fori(0, HT) as tile:
                        n = ((half * NE + e) * HT + tile) * FB
                        for f in range(FB):
                            act.wait_ge(gate_ps, n + f + 1)
                            act.wait_ge(lo_in, n + f - 1 + 2)
                            act.activation(g[:, f % 2, :], up1[f % 2][:, :], ACT.Silu).then_inc(gate_in, 1)
                            act.wait_ge(h_in, n + f + 1 + 2)
                            act.wait_ge(down_ps, n + (f - 2 if f >= 3 else 0) + 1)
                            act.copy(hs[:, f % 3, 0, :], g[:, f % 2, :]).then_inc(hi_in, 1)
                expert_loop(act, body)
                with act.Fori(0, RH // 2) as i:
                    for b in range(2):
                        act.wait_ge(ln_step, (half * RH + i * 2 + b) * 4 + 2)
                        act.activation(st[:, b, 10:11], st[:, b, 7:8], ACT.Sqrt, bias=eps[:, :]).then_inc(root, 1)

        @block.vector
        def _(dve):
            dve.sem_inc(h_in, 2)
            dve.sem_inc(lo_in, 2)
            dve.sem_inc(added, SUB)
            dve.wait_ge(set_in, 3)
            with dve.Fori(0, 2) as half:
                for c in range(DC):
                    dve.wait_ge(x_hi, half * DC + c + 1)
                    dve.tensor_tensor(xs[:, 1, c, :], raw[c][:, :], xs[:, 0, c, :].bitcast(F32), ALU.subtract).then_inc(split[c], 1)

                def body(e, i):
                    with dve.Fori(0, HT) as tile:
                        m = (half * NE + e) * HT + tile
                        for f in range(FB):
                            dve.wait_ge(up_ps, m * FB + f + 1)
                            dve.wait_ge(gate_in, m * FB + f + 1)
                            dve.tensor_tensor(g[:, f % 2, :], g[:, f % 2, :], up3[f % 2][:, :], ALU.mult).then_inc(h_in, 1)
                            dve.wait_ge(hi_in, m * FB + f + 1)
                            dve.tensor_tensor(hs[:, f % 3, 1, :], g[:, f % 2, :], hs[:, f % 3, 0, :].bitcast(F32), ALU.subtract).then_inc(lo_in, 1)
                        dve.wait_ge(acc_in, half * 16 + 16)
                        dve.wait_ge(down_ps, m * FB + FB + 1)
                        for q in range(SUB):
                            dve.wait_ge(added, m * SUB + q + 1)
                            r = ds(tile * SUB + q, 1)
                            dve.scalar_tensor_tensor(acc[:, r, :].rearrange("p o d -> p (o d)"), dn[q][:, 0:D],
                                                     gates_all[:, ds(half * RH + tile * SUB + q, 1), ds(e, 1)].rearrange("p o d -> p (o d)"),
                                                     acc[:, r, :].rearrange("p o d -> p (o d)"), ALU.mult, ALU.add).then_inc(added, 1)
                expert_loop(dve, body)
                with dve.Fori(0, RH // 2) as i:
                    for b in range(2):
                        k = (half * RH + i * 2 + b) * 4
                        row = acc[:, ds(i * 2 + b, 1), :].rearrange("p o d -> p (o d)")
                        s = st[:, b, :]
                        dve.wait_ge(added, (half * NE + NE) * (HT * SUB) + SUB)
                        dve.bn_stats(s[:, 0:6], row).then_inc(ln_step, 1)
                        dve.drain()
                        dve.bn_aggr(s[:, 6:8], s[:, 0:6]).then_inc(ln_step, 1)
                        dve.wait_ge(root, half * RH + i * 2 + b + 1)
                        dve.reciprocal(s[:, 11:12], s[:, 10:11]).then_inc(ln_step, 1)
                        dve.wait_ge(ln_step, k + 3)
                        dve.scalar_tensor_tensor(s[:, 12:13], s[:, 6:7], -1.0, s[:, 11:12], ALU.mult, ALU.mult).then_inc(ln_step, 1)
                        dve.wait_ge(ln_step, k + 4)
                        dve.wait_ge(y_out[b], half * (16 * RH // 2) + 16 * i + 16)
                        dve.tensor_scalar(y[:, b, :], row, s[:, 11:12], s[:, 12:13], ALU.mult, ALU.add).then_inc(y_in, 1)


def build(nc, io, dram, out):
    gates = nc.alloc_sbuf_tensor("gates", [P, T // P, NE], F32)
    attention(nc, io, dram, gates)
    experts(nc, io, dram, gates, out)


def kernel(**inputs):
    import numpy as _np
    import concourse.bacc as _bacc
    from concourse.bass_utils import run_bass_kernel_spmd as _run

    v = {k.split("_", 2)[2] if not k.startswith("L0_ffn") else k[len("L0_ffn_"):]: _np.asarray(x)
         for k, x in inputs.items()}

    def rows(m):
        return m.reshape(-1, P, m.shape[1]).transpose(1, 0, 2)

    perm = _np.concatenate([_np.arange(h * DK, h * DK + DK) for p in range(PR) for h in (p, p + PR)])
    x = v["x"][0]
    conv = _np.concatenate([
        _np.concatenate([v[n + "_w"][:, 0, :], v[n + "_b"][:, None]], 1)[o] for n, o in
        (("qc", perm), ("kc", perm), ("vc", _np.arange(H * DV)))])
    sel_v = _np.zeros((H, H, P), _np.float32)
    sel_p = _np.zeros((H, PR, P), _np.float32)
    for h in range(H):
        sel_v[h, h] = 1.0
        sel_p[h, h % PR, 64 * (h // PR):64 * (h // PR) + 64] = 1.0
    half_ones = _np.zeros((P, 2, P), _np.float32)
    half_ones[:DK, 0] = half_ones[DK:, 1] = 1.0
    arrays = dict(
        xT=rows(x.T), x=x.reshape(-1, P, D).transpose(1, 0, 2),
        wq=rows(v["Wq"].T[:, perm]), wk=rows(v["Wk"].T[:, perm]), wv=rows(v["Wv"].T), wa=rows(v["Wa"].T),
        wg=rows(v["Wg"].T), wo=rows(v["Wo"].T), wb=rows(v["Wb"].T), gw=rows(v["gate_W"].T),
        taps=conv.reshape(16, P, KC + 1).transpose(1, 0, 2), ba=v["ba"].reshape(H, P).T, bb=v["bb"][:, None],
        lnwb=_np.stack([v["ln_w"], v["ln_b"]], 1),
        ident=_np.eye(P, dtype=_np.float32), own_pair=_np.tile(_np.repeat(_np.eye(PR, dtype=_np.float32), CH, 0), (2, 1)), half_ones=half_ones,
        mean_w=_np.full((P, P), 1.0 / P, _np.float32), sel_v=sel_v, sel_p=sel_p,
        lower=_np.broadcast_to(_np.tril(_np.ones((E, E), _np.float32), -1).reshape(1, -1), (P, E * E)),
        eps=_np.full((P, 1), EPS, _np.float32),
        w1=_np.concatenate([v["w1_e"], v["w1_s"].transpose(1, 0, 2).reshape(1, D, FF)]).reshape(NE, DC, P, FF).transpose(2, 0, 1, 3),
        w3=_np.concatenate([v["w3_e"], v["w3_s"].transpose(1, 0, 2).reshape(1, D, FF)]).reshape(NE, DC, P, FF).transpose(2, 0, 1, 3),
        w2=_np.concatenate([v["w2_e"], v["w2_s"].reshape(1, FF, D)]).reshape(NE, FB, P, D).transpose(2, 0, 1, 3),
    )
    nc = _bacc.Bacc("TRN2", target_bir_lowering=False, num_devices=1)
    feeds, io = {}, {}
    for name, arr in arrays.items():
        arr = _np.ascontiguousarray(arr)
        feeds["in_" + name] = arr
        io[name] = nc.dram_tensor("in_" + name, arr.shape, mybir.dt.from_np(arr.dtype), kind="ExternalInput").ap()
    io["const_loads"] = [n for n in arrays if n not in ("x", "xT", "w1", "w3", "w2")]
    out = nc.dram_tensor("out0", (P, T // P, D), F32, kind="ExternalOutput").ap()
    dram = dict(x1=nc.dram_tensor("x1_d", (P, T // P, D), F32, kind="Internal").ap(),
                x1T=nc.dram_tensor("x1T_d", (P, DC, T), F32, kind="Internal").ap())
    build(nc, io, dram, out)
    got = _run(nc, [feeds], core_ids=[0]).results[0]["out0"]
    return got.transpose(1, 0, 2).reshape(1, T, D)
```

```python
from contextlib import ExitStack

import numpy as np
import concourse.bass as bass
from concourse import mybir

F32 = mybir.dt.float32
F32R = mybir.dt.float32r
ALU = mybir.AluOpType
ACT = mybir.ActivationFunctionType
X = mybir.AxisListType.X
ds = bass.ds

T, D = 4096, 256
H, DK, DV, KC = 8, 64, 128, 4
PR = H // 2
P = 128
DC = D // P
TT = 512
NT = T // TT
CH = 8
HC = CH // 2
BLK = HC * HC + HC * CH
UD = H * CH + H
NC = TT // CH
SL = CH + 1
E, FF = 8, 1024
NE = E + 1
FB = FF // P
SUB = TT // P
TH, HT = T // 2, NT // 2
RH = TH // P
EPS = 1e-5
SCALE = float(DK) ** -0.5
NF = 8 + 4 + 4 + 8
CREDIT = 2


def attention(nc, io, dram, gates_all):
    ctx = ExitStack()
    with ctx:
        def sb(name, shape):
            return ctx.enter_context(nc.sbuf_tensor(name, shape, F32))

        def sem(name):
            return ctx.enter_context(nc.semaphore(name))

        wq, wk = sb("wq", [P, DC, H * DK]), sb("wk", [P, DC, H * DK])
        wv, wa, wg = (sb(n, [P, DC, H * DV]) for n in ("wv", "wa", "wg"))
        wo = sb("wo", [P, H, D])
        wb = sb("wb", [P, DC, H])
        gw = sb("gw", [P, DC, E])
        taps = sb("taps", [P, 16, KC + 1])
        ba = sb("ba", [P, H])
        bb = sb("bb", [H, 1])
        lnwb = sb("lnwb", [P, 2])
        ident, mean_w = (sb(n, [P, P]) for n in ("ident", "mean_w"))
        half_ones = sb("half_ones", [P, 2, P])
        sel_v = sb("sel_v", [H, H, P])
        sel_p = sb("sel_p", [H, PR, P])
        sel_u = sb("sel_u", [UD, PR, P])
        lower = sb("lower", [P, E * E])
        eps = sb("eps", [P, 1])
        xT = sb("xT", [P, DC, TT])
        xt = sb("xt", [P, SUB, D])
        a = sb("a", [P, H, TT])
        bv = sb("bv", [P, H, TT])
        K = sb("K", [P, PR, TT])
        QK = sb("QK", [P, PR, 2, TT])
        oT = sb("oT", [P, H, TT])
        halo = sb("halo", [P, 16, KC - 1])
        raw = sb("raw", [P, 2, KC - 1 + TT])
        acc = sb("acc", [P, 2, TT])
        sil = sb("sil", [P, 2, TT])
        beta = sb("beta", [H, TT])
        R = sb("R", [P, 2, H, SL, SL])
        W = sb("W", [P, 2, H, 72])
        INV = sb("INV", [P, 2, H, 2, 16])
        inv_tmp = sb("inv_tmp", [P, H, 2, 3])
        prod_k = sb("prod_k", [P, 2, PR, BLK])
        prod_q = sb("prod_q", [P, 2, PR, BLK])
        kexp = sb("kexp", [P, H * CH])
        own_pair = sb("own_pair", [H * CH, PR])
        qkx = sb("qkx", [P, 2, PR, 2, 2, CH])
        Krow = sb("Krow", [H * CH, 2, PR, P])
        gq = sb("gq", [P, H, BLK])
        Nq = sb("Nq", [P, 2, H, BLK])
        rq = sb("rq", [P, H, CH])
        tree = sb("tree", [P, H, CH, 8])
        rsc = sb("rsc", [P, H, CH])
        c_in = sb("c_in", [P, H, CH])
        c_lo = sb("c_lo", [P, H, 4])
        P1 = sb("P1", [P, H, 4, 4])
        P2 = sb("P2", [P, H, 4, 5])
        c_hi = sb("c_hi", [P, H, 4])
        U = sb("U", [P, 2, H, CH])
        uF = sb("uF", [P, P])
        uT = sb("uT", [UD, P])
        S = sb("S", [P, 2, PR, P])
        SD = sb("SD", [P, PR, P])
        sq = acc
        sd = sil
        gt = raw
        x1 = sb("x1", [P, 2, D])
        x1T = sb("x1T", [P, 2, DC, P])
        stat = sb("stat", [P, 16])
        L = sb("L", [P, SUB, E])
        big = sb("big", [P, SUB, E, E])
        big2 = sb("big2", [P, SUB, E, E])
        small = sb("small", [P, 4, SUB])
        Lp = sb("Lp", [P, SUB, E])

        bank = [ctx.enter_context(nc.psum_tensor(f"bank{i}", [P, 512], F32)) for i in range(8)]
        g_k = bank[0][:, 0:H * BLK].rearrange("p (h e) -> p h e", h=H)
        g_q = bank[1][:, 0:H * BLK].rearrange("p (h e) -> p h e", h=H)
        k_row = bank[2][0:H * CH, 0:P]
        upd = [bank[i][:, 0:256].rearrange("p (r v) -> p r v", r=2) for i in (3, 7)]
        dbc = bank[4][:, :].rearrange("p (r v) -> p r v", r=PR)
        read = bank[5][:, 0:128].rearrange("p (h x t) -> p h x t", h=H, x=2)
        read_p = bank[5][:, 0:128].rearrange("p (g r y) -> p r g y", g=2, r=PR)
        u_row = bank[6][:, 0:P]

        def blocks(t):
            return (t[:, :, 0:HC * HC].rearrange("p h (t j) -> p h t j", t=HC),
                    t[:, :, HC * HC:BLK].rearrange("p h (t j) -> p h t j", t=HC))

        R81 = R[:, :, :, :, :].rearrange("p b h s r -> p b h (s r)")
        W64 = W[:, :, :, 0:64].rearrange("p b h (t j) -> p b h t j", t=CH)
        W36 = W[:, :, :, :].rearrange("p b h (k r) -> p b h k r", k=2)

        loaded = sem("loaded")
        ready_set = sem("ready_set")
        xT_in = sem("xT_in")
        xt_in = sem("xt_in")
        stored = [sem(f"stored{i}") for i in range(2)]
        beta_logit = sem("beta_logit")
        beta_sig = sem("beta_sig")
        projected = sem("projected")
        evacuated = sem("evacuated")
        raw_in = sem("raw_in")
        tap = sem("tap")
        halo_in = sem("halo_in")
        conv_done = sem("conv_done")
        silu_done = sem("silu_done")
        beta_bc = sem("beta_bc")
        beta_used = sem("beta_used")
        key_step = sem("key_step")
        tile_in = sem("tile_in")
        names = ("upd_a_ps", "state_a_in", "slots_in", "rq_in", "qkx_in", "kexp_in", "krow_in", "gq_in", "ut_in", "dcol_in",
                 "prodk", "prodq", "w_in", "sd_in", "u_in", "uf_in", "state_in",
                 "gramk", "gramq", "krow_ps", "reads_ps", "ut_ps", "dbc_ps", "upd_ps",
                 "nq_in", "o_in", "rs_in", "decays_in", "inv_in", "c_in_s")
        s = {n: sem("s_" + n) for n in names}
        first_ps, first_in = sem("first_ps"), sem("first_in")
        decay_step = sem("decay_step")
        inv_step = sem("inv_step")
        sub_step = sem("sub_step")
        out_step = sem("out_step")
        mean_ps, centred, squared, var_ps, sd_in, normed = (sem(n) for n in (
            "mean_ps", "centred", "squared", "var_ps", "sd_root", "normed"))
        rstd_in = sem("rstd_in")
        gate_ps, gate_in, affine, gated = (sem(n) for n in ("gate_ps", "gate_in", "affine", "gated"))
        y_ps, resid, ln_step, ln_root, x1_in = (sem(n) for n in ("y_ps", "resid", "ln_step", "ln_root", "x1_in"))
        xT_ps, x1T_in, logit_ps = (sem(n) for n in ("xT_ps", "x1T_in", "logit_ps"))
        route_step, route_max, route_exp, routed = (sem(n) for n in ("route_step", "route_max", "route_exp", "routed"))

        block = ctx.enter_context(nc.Block())
        n_loads = len(io["const_loads"])
        consts = dict(wq=wq, wk=wk, wv=wv, wa=wa, wg=wg, wo=wo, wb=wb, gw=gw, taps=taps, ba=ba, bb=bb,
                      lnwb=lnwb, ident=ident, own_pair=own_pair, half_ones=half_ones, mean_w=mean_w, sel_v=sel_v, sel_p=sel_p,
                      sel_u=sel_u, lower=lower, eps=eps)

        def chunk_loop(eng, tile, first, step):
            first(tile)
            with eng.Fori(0, NC // 4 - 1) as i:
                for b in range(4):
                    step(tile * NC + i * 4 + b, i * 4 + b, b % 2, 2)
            for b, left in enumerate((2, 2, 1, 0)):
                step(tile * NC + NC - 4 + b, NC - 4 + b, b % 2, left)

        @block.sync
        def _(sp):
            for name in io["const_loads"]:
                t = consts[name]
                sp.dma_start(t.ap(), io[name]).then_inc(loaded, 16)
            for b in range(2):
                sp.sem_inc(stored[b], 32)
            with sp.Fori(0, NT) as tile:
                sp.wait_ge(gate_ps, tile * H + 1)
                sp.dma_start(xT[:, :, :], io["xT"][:, :, ds(tile * TT, TT)]).then_inc(xT_in, 16)
                sp.dma_start(xt[:, :, :], io["x"][:, ds(tile * SUB, SUB), :]).then_inc(xt_in, 16)
                for q in range(SUB):
                    sp.wait_ge(x1_in, tile * SUB + q + 1)
                    sp.dma_start(dram["x1"][:, ds(tile * SUB + q, 1), :], x1[:, q % 2:q % 2 + 1, :]).then_inc(stored[q % 2], 16)
                    sp.wait_ge(x1T_in, tile * SUB + q + 1)
                    sp.dma_start(dram["x1T"][:, :, ds(tile * TT + q * P, P)], x1T[:, q % 2, :, :]).then_inc(stored[q % 2], 16)
            for b in range(2):
                sp.wait_ge(stored[b], 32 * (NT * SUB // 2 + 1))

        @block.gpsimd
        def _(pool):
            for t in (kexp[:, :], qkx[:, :, :, :, :, :], halo[:, :, :], S[:, :, :, :], INV[:, :, :, :, :], uF[:, :]):
                pool.memset(t, 0.0).then_inc(ready_set, 1)
            pool.memset(R81[:, :, :, :], 0.0).then_inc(ready_set, 1)
            pool.wait_ge(ready_set, 7)
            pool.memset(R81[:, :, :, 0:81:10], 1.0).then_inc(ready_set, 1)
            pool.memset(INV[:, :, :, :, 0:16:5], 1.0).then_inc(ready_set, 1)
            pool.wait_ge(ready_set, 9)

            def weigh(n, c, b):
                pool.wait_ge(s["gq_in"], n + 1 + CREDIT)
                pool.wait_ge(s["decays_in"], n + 1 + CREDIT)
                for i, (nq, g) in enumerate(zip(blocks(Nq[:, b]), blocks(gq))):
                    k = pool.tensor_tensor(nq, g, R[:, b, :, 1:1 + HC * (i + 1), 1 + HC * i:1 + HC * (i + 1)]
                                           .rearrange("p h j t -> p h t j"), ALU.mult)
                k.then_inc(s["nq_in"], 1)

            def outputs(n, c, b):
                pool.wait_ge(s["rq_in"], n + 1 + CREDIT)
                pool.wait_ge(s["o_in"], n + CREDIT)
                pool.tensor_tensor(rsc[:, :, :], rq[:, :, :], R[:, b, :, 0, 1:SL], ALU.mult).then_inc(s["rs_in"], 1)
                pool.wait_ge(s["u_in"], n + 1 + CREDIT)
                pool.wait_ge(s["nq_in"], n + 1 + CREDIT)
                at = lambda k: n * 5 + k + CREDIT * 5
                lo, hi = blocks(Nq[:, b])
                pool.tensor_tensor(tree[:, :, 0:HC, 0:4], lo, U[:, b, :, 0:HC].unsqueeze(2).to_broadcast([P, H, HC, HC]), ALU.mult).then_inc(out_step, 1)
                pool.tensor_tensor(hi, hi, U[:, b].unsqueeze(2).to_broadcast([P, H, HC, CH]), ALU.mult).then_inc(out_step, 1)
                pool.wait_ge(out_step, at(2))
                pool.tensor_tensor(tree[:, :, HC:CH, 0:4], hi[:, :, :, 0:4], hi[:, :, :, 4:8], ALU.add).then_inc(out_step, 1)
                pool.wait_ge(out_step, at(3))
                pool.tensor_tensor(tree[:, :, :, 4:6], tree[:, :, :, 0:2], tree[:, :, :, 2:4], ALU.add).then_inc(out_step, 1)
                pool.wait_ge(out_step, at(4))
                pool.wait_ge(s["rs_in"], n + 1 + CREDIT)
                pool.tensor_tensor(tree[:, :, :, 6], tree[:, :, :, 4], tree[:, :, :, 5], ALU.add).then_inc(out_step, 1)
                pool.wait_ge(out_step, at(5))
                pool.tensor_tensor(oT[:, :, ds(c * CH, CH)], tree[:, :, :, 6], rsc[:, :, :], ALU.add).then_inc(s["o_in"], 1)

            def step(n, c, b, left):
                outputs(n, c, b)
                if left:
                    weigh(n + 1, c + 1, 1 - b)

            pool.sem_inc(out_step, 5 * CREDIT)
            for name in ("nq_in", "rs_in", "o_in"):
                pool.sem_inc(s[name], CREDIT)
            with pool.Fori(0, NT) as tile:
                pool.wait_ge(gated, tile * H + 2)
                pool.wait_ge(y_ps, tile * SUB + 1)
                chunk_loop(pool, tile, lambda tile: weigh(tile * NC, 0, 0), step)

        @block.scalar
        def _(act):
            def conv_part(tile, f):
                e = 8 + f
                act.wait_ge(projected, tile * NF + e + 1)
                act.wait_ge(conv_done, tile * 16 + f - 1 + 2)
                act.wait_ge(silu_done, tile * 16 + f - 1 + 2)
                act.copy(raw[:, f % 2, KC - 1:], bank[e % 2][:, :]).then_inc(raw_in, 1)
                act.activation(acc[:, f % 2, :], bank[e % 2][:, :], ACT.Identity, bias=taps[:, f, KC:KC + 1],
                               scale=taps[:, f, KC - 1:KC]).then_inc(evacuated, 1)

            def silu_part(tile, f):
                act.wait_ge(conv_done, tile * 16 + f + 1 + 2)
                if f >= 4:
                    act.wait_ge(beta_used, tile * 12 + f - 4 - 1 + 2)
                dst = QK[:, f, 1, :] if f < 4 else sil[:, f % 2, :]
                act.activation(dst, acc[:, f % 2, :], ACT.Silu).then_inc(silu_done, 1)

            def prepare(n, c, b):
                act.wait_ge(s["uf_in"], n - 1 + CREDIT)
                act.wait_ge(s["rs_in"], n - 1 + CREDIT)
                act.wait_ge(s["w_in"], n - 1 + CREDIT)
                act.copy(R81[:, b, :, 1:72:10], a[:, :, ds(c * CH, CH)]).then_inc(s["slots_in"], 1)

            def stage(n, c, b):
                act.wait_ge(s["reads_ps"], n - 1 + CREDIT)
                for half in range(2):
                    r = slice(64 * half, 64 * half + 64)
                    i = act.copy(qkx[r, b, :, half, :, :], QK[r, :, :, ds(c * CH, CH)])
                i.then_inc(s["qkx_in"], 1)
                act.wait_ge(s["krow_ps"], n + CREDIT)
                for half in range(2):
                    r = slice(64 * half, 64 * half + 64)
                    i = act.copy(kexp[r, 32 * half:32 * half + 32].rearrange("p (r t) -> p r t", r=PR), K[r, :, ds(c * CH, CH)])
                i.then_inc(s["kexp_in"], 1)

            def decay_column(n, c, b):
                act.wait_ge(s["decays_in"], n + 1 + CREDIT)
                act.wait_ge(s["ut_ps"], n - 1 + CREDIT)
                act.copy(uF[:, H * CH:UD], R[:, b, :, 0, CH]).then_inc(s["dcol_in"], 1)

            def rows(n):
                act.wait_ge(s["upd_ps"], n + CREDIT)
                return act.copy(uT[:, :], u_row[0:UD, :])

            def finish(n, c, b):
                act.wait_ge(s["krow_ps"], n + 1 + CREDIT)
                act.wait_ge(s["upd_ps"], n - 1 + CREDIT)
                for p in range(PR):
                    i = act.activation(Krow[:, b, p, :], k_row, ACT.Identity, scale=own_pair[:, p:p + 1])
                i.then_inc(s["krow_in"], 1)
                act.wait_ge(s["gramq"], n + 1 + CREDIT)
                act.wait_ge(s["nq_in"], n + CREDIT)
                act.copy(gq[:, :, :], g_q).then_inc(s["gq_in"], 1)

            def first(tile):
                n, c, b = tile * NC, 0, 0
                prepare(n, c, b)
                stage(n, c, b)
                decay_column(n, c, b)
                act.wait_ge(first_ps, tile + 1)
                act.wait_ge(s["dbc_ps"], n + CREDIT)
                rows(n).then_inc(first_in, 1)
                finish(n, c, b)
                prepare(n + 1, c + 1, 1 - b)

            def step(n, c, b, left):
                act.wait_ge(s["c_in_s"], n + 1 + CREDIT)
                act.wait_ge(s["rs_in"], n + CREDIT)
                act.copy(rq[:, :, :], read[:, :, 1, :]).then_inc(s["rq_in"], 1)
                if left:
                    stage(n + 1, c + 1, 1 - b)
                    decay_column(n + 1, c + 1, 1 - b)
                act.wait_ge(s["ut_ps"], n + 1 + CREDIT)
                act.wait_ge(s["dbc_ps"], n + 1 + CREDIT)
                rows(n).then_inc(s["ut_in"], 1)
                if left:
                    finish(n + 1, c + 1, 1 - b)
                if left == 2:
                    prepare(n + 2, c + 2, b)

            act.wait_ge(loaded, 16 * n_loads)
            act.wait_ge(ready_set, 9)
            for name in ("slots_in", "rq_in", "qkx_in", "kexp_in", "krow_in", "gq_in", "ut_in", "dcol_in"):
                act.sem_inc(s[name], CREDIT)
            act.sem_inc(silu_done, 2)
            with act.Fori(0, NT) as tile:
                act.wait_ge(beta_logit, tile + 1)
                act.activation(beta[:, :], bank[4][0:H, :], ACT.Sigmoid, bias=bb[:, :]).then_inc(beta_sig, 1)
                for e in range(H):
                    act.wait_ge(projected, tile * NF + e + 1)
                    act.activation(a[:, e, :], bank[e % 2][:, :], ACT.Sigmoid, bias=ba[:, e:e + 1]).then_inc(evacuated, 1)
                for f in range(16):
                    conv_part(tile, f)
                    if f:
                        silu_part(tile, f - 1)
                silu_part(tile, 15)
                act.wait_ge(tile_in, tile + 1)
                act.wait_ge(silu_done, tile * 16 + 16 + 2)
                chunk_loop(act, tile, first, step)
                for h in range(H):
                    act.wait_ge(centred, tile * H + h + 1)
                    act.wait_ge(var_ps, tile * H + h - 1 + 2)
                    act.activation(sq[:, h % 2, :], oT[:, h, :], ACT.Square).then_inc(squared, 1)
                    act.wait_ge(var_ps, tile * H + h + 1 + 2)
                    act.wait_ge(rstd_in, tile * H + h - 1 + 2)
                    act.activation(sd[:, h % 2, :], bank[2 + h % 2][:, :], ACT.Sqrt, bias=eps[:, :]).then_inc(sd_in, 1)
                for h in range(H):
                    act.wait_ge(gate_ps, tile * H + h + 1 + 1)
                    act.wait_ge(gated, tile * H + h - 1 + 2)
                    act.activation(gt[:, h % 2, 0:TT], bank[4 + h % 2][:, :], ACT.Sigmoid).then_inc(gate_in, 1)
                for q in range(SUB):
                    act.wait_ge(ln_step, (tile * SUB + q) * 4 + 2)
                    act.activation(stat[:, 10:11], stat[:, 7:8], ACT.Sqrt, bias=eps[:, :]).then_inc(ln_root, 1)
                    act.wait_ge(xT_ps, tile * SUB + q + 1 + 2)
                    act.wait_ge(stored[q % 2], 32 * (tile * 2 + q // 2 + 1))
                    act.wait_ge(logit_ps, tile * SUB + q - 1 + 2)
                    act.copy(x1T[:, q % 2], bank[0][:, 0:D].rearrange("p (c t) -> p c t", c=DC)).then_inc(x1T_in, 1)
                act.wait_ge(route_max, tile + 1)
                act.activation(Lp[:, :, :], L[:, :, :], ACT.Exp).then_inc(route_exp, 1)

        @block.tensor
        def _(pe):
            mm, tr = pe.matmul, pe.transpose

            def project(out, w, e):
                for c in range(DC):
                    i = mm(out, w[:, c, e * P:(e + 1) * P], xT[:, c, :], start=c == 0, stop=c == DC - 1)
                return i

            def grams_k(n, b):
                pe.wait_ge(s["prodk"], n + 1 + CREDIT)
                pe.wait_ge(s["w_in"], n + CREDIT)
                for half in range(2):
                    i = mm(g_k[:, 4 * half:4 * half + 4], half_ones[:, half, :], prod_k[:, b], start=True, stop=True)
                i.then_inc(s["gramk"], 1)

            def grams_q(n, b, half):
                if half == 0:
                    pe.wait_ge(s["prodq"], n + 1 + CREDIT)
                    pe.wait_ge(s["gq_in"], n + CREDIT)
                i = mm(g_q[:, 4 * half:4 * half + 4], half_ones[:, half, :], prod_q[:, b], start=True, stop=True)
                if half == 1:
                    i.then_inc(s["gramq"], 1)

            def key_rows(n, c, b):
                tr(k_row, kexp[:, :], ident[:, :]).then_inc(s["krow_ps"], 1)

            def decay_bc(n):
                pe.wait_ge(s["ut_in"], n + CREDIT)
                pe.wait_ge(s["sd_in"], n + CREDIT)
                for p in range(PR):
                    i = mm(dbc[:, p, :], sel_u[H * CH:UD, p, :], uT[H * CH:UD, :], start=True, stop=True)
                i.then_inc(s["dbc_ps"], 1)

            def first(tile):
                n, c, b = tile * NC, 0, 0
                grams_k(n, b)
                grams_q(n, b, 0)
                pe.wait_ge(s["kexp_in"], n + 1 + CREDIT)
                pe.wait_ge(s["krow_in"], n + CREDIT)
                pe.wait_ge(s["dcol_in"], n + 1 + CREDIT)
                pe.wait_ge(s["ut_in"], n + CREDIT)
                tr(u_row, uF[:, :], ident[:, :]).then_inc(first_ps, 1)
                key_rows(n, c, b)
                pe.wait_ge(first_in, tile + 1)
                grams_q(n, b, 1)

            def step(n, c, b, left):
                pe.wait_ge(s["qkx_in"], n + 1 + CREDIT)
                pe.wait_ge(s["rq_in"], n + CREDIT)
                pe.wait_ge(s["c_in_s"], n + CREDIT)
                for p in range(PR):
                    if p % 2 == 0:
                        pe.wait_ge(s["state_a_in" if p == 0 else "state_in"], n + CREDIT)
                    i = mm(read_p[:, p], S[:, b, p, :], qkx[:, b, p].rearrange("p g x t -> p (g x t)"), start=True, stop=True)
                i.then_inc(s["reads_ps"], 1)
                decay_bc(n)
                if left:
                    grams_k(n + 1, 1 - b)
                    grams_q(n + 1, 1 - b, 0)
                pe.wait_ge(s["uf_in"], n + 1 + CREDIT)
                if left:
                    pe.wait_ge(s["dcol_in"], n + 2 + CREDIT)
                tr(u_row, uF[:, :], ident[:, :]).then_inc(s["ut_ps"], 1)
                if left:
                    grams_q(n + 1, 1 - b, 1)
                    pe.wait_ge(s["kexp_in"], n + 2 + CREDIT)
                pe.wait_ge(s["ut_in"], n + 1 + CREDIT)
                pe.wait_ge(s["krow_in"], n + 1 + CREDIT)
                for p in range(PR):
                    i = mm(upd[p // 2][:, p % 2, :], Krow[:, b, p, :], uT[0:H * CH, :], start=True, stop=True)
                    if p == 1:
                        i.then_inc(s["upd_a_ps"], 1)
                i.then_inc(s["upd_ps"], 1)
                if left:
                    key_rows(n + 1, c + 1, 1 - b)

            pe.wait_ge(loaded, 16 * n_loads)
            pe.wait_ge(ready_set, 9)
            for name in ("upd_a_ps", "gramk", "gramq", "krow_ps", "reads_ps", "ut_ps", "dbc_ps", "upd_ps"):
                pe.sem_inc(s[name], CREDIT)
            pe.sem_inc(gate_ps, 1)
            pe.sem_inc(y_ps, 1)
            pe.sem_inc(var_ps, 2)
            pe.sem_inc(xT_ps, 2)
            pe.sem_inc(logit_ps, 2)
            with pe.Fori(0, NT) as tile:
                pe.wait_ge(xT_in, 16 * tile + 16)
                pe.wait_ge(routed, tile + 1)
                for c in range(DC):
                    i = mm(bank[4][0:H, :], wb[:, c, :], xT[:, c, :], start=c == 0, stop=c == DC - 1)
                i.then_inc(beta_logit, 1)
                parts = [(wa, h) for h in range(H)] + [(wq, p) for p in range(PR)] + [(wk, p) for p in range(PR)]\
                    + [(wv, h) for h in range(H)]
                for e, (w, j) in enumerate(parts):
                    if e >= 2:
                        pe.wait_ge(evacuated, tile * NF + e - 1)
                    project(bank[e % 2][:, :], w, j).then_inc(projected, 1)
                    if e >= 12:
                        j = e - 12
                        if j == 0:
                            pe.wait_ge(beta_sig, tile + 1)
                        pe.wait_ge(beta_used, tile * 12 + j - 1 + 2)
                        sel = sel_p[:, j, :] if j < PR else sel_v[:, j - PR, :]
                        mm(bank[2 + j % 2][:, :], sel, beta[:, :], start=True, stop=True).then_inc(beta_bc, 1)
                pe.wait_ge(evacuated, tile * NF + NF)
                pe.wait_ge(tile_in, tile + 1)
                chunk_loop(pe, tile, first, step)
                pe.wait_ge(s["o_in"], tile * NC + NC + CREDIT)
                pe.wait_ge(s["state_in"], tile * NC + NC + CREDIT)

                def variance(h):
                    pe.wait_ge(squared, tile * H + h + 1)
                    pe.wait_ge(sd_in, tile * H + h - 1 + 2)
                    mm(bank[2 + h % 2][:, :], mean_w[:, :], sq[:, h % 2, :], start=True, stop=True).then_inc(var_ps, 1)
                for h in range(H):
                    if h >= 2:
                        pe.wait_ge(centred, tile * H + h - 1)
                    mm(bank[h % 2][:, :], mean_w[:, :], oT[:, h, :], start=True, stop=True).then_inc(mean_ps, 1)
                    if h:
                        variance(h - 1)
                variance(H - 1)
                for h in range(H):
                    if h >= 2:
                        pe.wait_ge(gate_in, tile * H + h - 1)
                    project(bank[4 + h % 2][:, :], wg, h).then_inc(gate_ps, 1)

                def transposes(q):
                    pe.wait_ge(x1_in, tile * SUB + q + 1)
                    if q:
                        pe.wait_ge(x1T_in, tile * SUB + q)
                    else:
                        pe.wait_ge(normed, tile + 1)
                    for c in range(DC):
                        i = tr(bank[0][:, c * P:(c + 1) * P], x1[:, q % 2, c * P:(c + 1) * P], ident[:, :])
                    i.then_inc(xT_ps, 1)

                def logits(q):
                    pe.wait_ge(x1T_in, tile * SUB + q + 1)
                    for c in range(DC):
                        i = mm(bank[1][:, q * E:(q + 1) * E], x1T[:, q % 2, c, :], gw[:, c, :], start=c == 0, stop=c == DC - 1)
                    i.then_inc(logit_ps, 1)
                pe.wait_ge(gated, tile * H + H + 2)
                for q in range(SUB):
                    if q >= 2:
                        pe.wait_ge(resid, tile * SUB + q - 1 + 1)
                    for h in range(H):
                        i = mm(bank[6 + q % 2][:, 0:D], oT[:, h, q * P:(q + 1) * P], wo[:, h, :], start=h == 0, stop=h == H - 1)
                    i.then_inc(y_ps, 1)
                for q in range(SUB):
                    transposes(q)
                    logits(q)

        @block.vector
        def _(dve):
            tt, stt = dve.tensor_tensor, dve.scalar_tensor_tensor

            def conv(tile, f):
                b = f % 2
                dve.tensor_copy(raw[:, b, 0:KC - 1], halo[:, f, :]).then_inc(halo_in, 1)
                dve.wait_ge(halo_in, tile * 16 + f + 1)
                dve.wait_ge(raw_in, tile * 16 + f + 1)
                dve.wait_ge(evacuated, tile * NF + 8 + f + 1)
                for k in range(KC - 1):
                    if k:
                        dve.wait_ge(tap, tile * 48 + 3 * f + k)
                    i = stt(acc[:, b, :], raw[:, b, k:k + TT], taps[:, f, k:k + 1], acc[:, b, :], ALU.mult, ALU.add)
                    i.then_inc(tap, 1)
                dve.wait_ge(tap, tile * 48 + 3 * f + 3)
                dve.tensor_copy(halo[:, f, :], raw[:, b, TT:]).then_inc(conv_done, 1)

            def use_beta(tile, f):
                j = f - 4
                dve.wait_ge(silu_done, tile * 16 + f + 1 + 2)
                dve.wait_ge(beta_bc, tile * 12 + j + 1)
                ps = bank[2 + j % 2][:, :]
                if j < PR:
                    dve.tensor_scalar(K[:, j, :], sil[:, f % 2, :], SCALE, None, ALU.mult).then_inc(key_step, 1)
                    stt(QK[:, j, 0, :], sil[:, f % 2, :], -SCALE, ps, ALU.mult, ALU.mult).then_inc(beta_used, 1)
                else:
                    tt(bv[:, j - PR, :], sil[:, f % 2, :], ps, ALU.mult).then_inc(beta_used, 1)

            def decays_a(n, c, b):
                dve.wait_ge(s["slots_in"], n + 1 + CREDIT)
                tt(R81[:, b, :, 2:63:20], R81[:, b, :, 1:62:20], R81[:, b, :, 11:72:20], ALU.mult).then_inc(decay_step, 1)

            def decays_b(n, c, b):
                dve.wait_ge(decay_step, n * 3 + 1)
                for o in (0, 4):
                    tt(R[:, b, :, o:o + 2, o + 3:o + 5], R[:, b, :, o:o + 2, o + 2:o + 3].to_broadcast([P, H, 2, 2]),
                       R[:, b, :, o + 2:o + 3, o + 3:o + 5].to_broadcast([P, H, 2, 2]), ALU.mult).then_inc(decay_step, 1)

            def decays_c(n, c, b):
                dve.wait_ge(decay_step, n * 3 + 3)
                tt(R[:, b, :, 0:4, 5:9], R[:, b, :, 0:4, 4:5].to_broadcast([P, H, 4, 4]),
                   R[:, b, :, 4:5, 5:9].to_broadcast([P, H, 4, 4]), ALU.mult).then_inc(s["decays_in"], 1)

            def products(n, c, b, x, out, made, used):
                dve.wait_ge(s[used], n - 1 + CREDIT)
                for i, o in enumerate(blocks(out[:, b])):
                    q, k = ds(c * CH + HC * i, HC), ds(c * CH, HC * (i + 1))
                    m = tt(o, QK[:, :, x, q].unsqueeze(3).to_broadcast([P, PR, HC, HC * (i + 1)]),
                           K[:, :, k].unsqueeze(2).to_broadcast([P, PR, HC, HC * (i + 1)]), ALU.mult)
                m.then_inc(s[made], 1)

            def weights(n, c, b):
                dve.wait_ge(s["gramk"], n + 1 + CREDIT)
                dve.wait_ge(s["decays_in"], n + 1 + CREDIT)
                lo, hi = blocks(g_k)
                for w, g, r in ((W64[:, b, :, 1:4, 0:3], lo[:, :, 1:4, 0:3], R[:, b, :, 1:4, 1:4]),
                                (W64[:, b, :, 4:8, 0:7], hi[:, :, :, 0:7], R[:, b, :, 1:8, 4:8])):
                    i = tt(w, g, r.rearrange("p h j t -> p h t j"), ALU.mult)
                i.then_inc(s["w_in"], 1)

            def inverses(n, c, b):
                w, v, m = W36[:, b], INV[:, b], inv_tmp
                dve.wait_ge(s["w_in"], n + 1 + CREDIT)
                dve.tensor_copy(v[:, :, :, 4:15:5], w[:, :, :, 8:27:9]).then_inc(inv_step, 1)
                tt(m[:, :, :, 0:2], w[:, :, :, 17:27:9], w[:, :, :, 8:18:9], ALU.mult).then_inc(inv_step, 1)
                dve.wait_ge(inv_step, n * 5 + 2)
                tt(v[:, :, :, 8:14:5], m[:, :, :, 0:2], w[:, :, :, 16:26:9], ALU.add).then_inc(inv_step, 1)
                dve.wait_ge(inv_step, n * 5 + 3)
                tt(m[:, :, :, 0:2], w[:, :, :, 25:27], v[:, :, :, 4:9:4], ALU.mult).then_inc(inv_step, 1)
                dve.wait_ge(inv_step, n * 5 + 4)
                tt(m[:, :, :, 2], m[:, :, :, 0], m[:, :, :, 1], ALU.add).then_inc(inv_step, 1)
                dve.wait_ge(inv_step, n * 5 + 5)
                tt(v[:, :, :, 12], m[:, :, :, 2], w[:, :, :, 24], ALU.add).then_inc(s["inv_in"], 1)

            def first(tile):
                n, c, b = tile * NC, 0, 0
                decays_a(n, c, b)
                products(n, c, b, 0, prod_k, "prodk", "gramk")
                decays_b(n, c, b)
                products(n, c, b, 1, prod_q, "prodq", "gramq")
                decays_c(n, c, b)
                weights(n, c, b)
                inverses(n, c, b)
                products(n + 1, c + 1, 1 - b, 0, prod_k, "prodk", "gramk")
                products(n + 1, c + 1, 1 - b, 1, prod_q, "prodq", "gramq")

            def step(n, c, b, left):
                at = lambda k: n * 7 + k
                m = (n + 1, c + 1, 1 - b)
                dve.wait_ge(s["reads_ps"], n + 1 + CREDIT)
                tt(c_in[:, :, :], read[:, :, 0, :], R[:, b, :, 0, 0:CH], ALU.mult).then_inc(s["c_in_s"], 1)
                if left:
                    decays_a(*m)
                dve.wait_ge(s["c_in_s"], n + 1 + CREDIT)
                tt(c_lo[:, :, :], c_in[:, :, 0:4], bv[:, :, ds(c * CH, 4)], ALU.add).then_inc(sub_step, 1)
                tt(P2[:, :, :, 4], c_in[:, :, 4:8], bv[:, :, ds(c * CH + 4, 4)], ALU.add).then_inc(sub_step, 1)
                if left:
                    decays_b(*m)
                dve.wait_ge(sub_step, at(1))
                dve.wait_ge(s["inv_in"], n + 1 + CREDIT)
                tt(P1[:, :, :, :], INV[:, b, :, 0, :].rearrange("p h (t j) -> p h t j", t=4),
                   c_lo[:, :, :].unsqueeze(2).to_broadcast([P, H, 4, 4]), ALU.mult).then_inc(sub_step, 1)
                if left:
                    decays_c(*m)
                dve.wait_ge(sub_step, at(3))
                dve.wait_ge(s["o_in"], n - 1 + CREDIT)
                dve.tensor_reduce(U[:, b, :, 0:4], P1[:, :, :, :], X, ALU.add).then_inc(sub_step, 1)
                dve.wait_ge(sub_step, at(4))
                tt(P2[:, :, :, 0:4], W64[:, b, :, 4:8, 0:4], U[:, b, :, 0:4].unsqueeze(2).to_broadcast([P, H, 4, 4]),
                   ALU.mult).then_inc(sub_step, 1)
                dve.wait_ge(sub_step, at(5))
                dve.tensor_reduce(c_hi[:, :, :], P2[:, :, :, :], X, ALU.add).then_inc(sub_step, 1)
                dve.wait_ge(sub_step, at(6))
                tt(P1[:, :, :, :], INV[:, b, :, 1, :].rearrange("p h (t j) -> p h t j", t=4),
                   c_hi[:, :, :].unsqueeze(2).to_broadcast([P, H, 4, 4]), ALU.mult).then_inc(sub_step, 1)
                dve.wait_ge(sub_step, at(7))
                dve.tensor_reduce(U[:, b, :, 4:8], P1[:, :, :, :], X, ALU.add).then_inc(s["u_in"], 1)
                dve.wait_ge(s["u_in"], n + 1 + CREDIT)
                dve.wait_ge(s["ut_ps"], n + CREDIT)
                tt(uF[:, 0:H * CH].rearrange("p (h t) -> p h t", h=H), U[:, b], R[:, b, :, 1:SL, CH], ALU.mult).then_inc(s["uf_in"], 1)
                dve.wait_ge(s["dbc_ps"], n + 1 + CREDIT)
                tt(SD[:, :, :], S[:, b], dbc, ALU.mult).then_inc(s["sd_in"], 1)
                if left:
                    weights(*m)
                if left == 2:
                    products(n + 2, c + 2, b, 0, prod_k, "prodk", "gramk")
                    products(n + 2, c + 2, b, 1, prod_q, "prodq", "gramq")
                dve.wait_ge(s["upd_a_ps"], n + 1 + CREDIT)
                dve.wait_ge(s["sd_in"], n + 1 + CREDIT)
                tt(S[:, 1 - b, 0:2], SD[:, 0:2], upd[0], ALU.add).then_inc(s["state_a_in"], 1)
                dve.wait_ge(s["upd_ps"], n + 1 + CREDIT)
                tt(S[:, 1 - b, 2:4], SD[:, 2:4], upd[1], ALU.add).then_inc(s["state_in"], 1)
                if left:
                    inverses(*m)

            for name in ("prodk", "prodq", "w_in", "sd_in", "u_in", "uf_in", "state_in", "state_a_in", "decays_in", "inv_in", "c_in_s"):
                dve.sem_inc(s[name], CREDIT)
            for x, v in ((conv_done, 2), (beta_used, 2), (gated, 2), (resid, 1), (rstd_in, 2), (routed, 1), (sd_in, 2)):
                dve.sem_inc(x, v)
            dve.wait_ge(loaded, 16 * n_loads)
            dve.wait_ge(ready_set, 9)
            with dve.Fori(0, NT) as tile:
                for f in range(16):
                    conv(tile, f)
                    if f > 4:
                        use_beta(tile, f - 1)
                use_beta(tile, 15)
                dve.drain().then_inc(tile_in, 1)
                dve.wait_ge(silu_done, tile * 16 + 16 + 2)
                dve.wait_ge(tile_in, tile + 1)
                chunk_loop(dve, tile, first, step)
                dve.wait_ge(s["o_in"], tile * NC + NC + CREDIT)

                def centre(h):
                    dve.wait_ge(mean_ps, tile * H + h + 1)
                    tt(oT[:, h, :], oT[:, h, :], bank[h % 2][:, :], ALU.subtract).then_inc(centred, 1)

                def scale_(h):
                    dve.wait_ge(sd_in, tile * H + h + 1 + 2)
                    dve.reciprocal(sd[:, h % 2, :], sd[:, h % 2, :]).then_inc(route_step, 1)
                    dve.wait_ge(route_step, tile * (H + 11) + h + 1)
                    dve.wait_ge(squared, tile * H + h + 1)
                    tt(oT[:, h, :], oT[:, h, :], sd[:, h % 2, :], ALU.mult).then_inc(rstd_in, 1)
                for h in range(H):
                    centre(h)
                    if h:
                        scale_(h - 1)
                scale_(H - 1)
                dve.drain().then_inc(normed, 1)
                for h in range(H):
                    dve.tensor_scalar(oT[:, h, :], oT[:, h, :], lnwb[:, 0:1], lnwb[:, 1:2], ALU.mult, ALU.add).then_inc(affine, 1)
                    dve.wait_ge(affine, tile * H + h + 1)
                    dve.wait_ge(gate_in, tile * H + h + 1)
                    tt(oT[:, h, :], oT[:, h, :], gt[:, h % 2, 0:TT], ALU.mult).then_inc(gated, 1)
                dve.wait_ge(xt_in, 16 * tile + 16)
                for q in range(SUB):
                    k = (tile * SUB + q) * 4
                    dve.wait_ge(y_ps, tile * SUB + q + 1 + 1)
                    tt(xt[:, q, :], xt[:, q, :], bank[6 + q % 2][:, 0:D], ALU.add).then_inc(resid, 1)
                    dve.wait_ge(resid, tile * SUB + q + 1 + 1)
                    dve.bn_stats(stat[:, 0:6], xt[:, q, :]).then_inc(ln_step, 1)
                    dve.drain()
                    dve.bn_aggr(stat[:, 6:8], stat[:, 0:6]).then_inc(ln_step, 1)
                    dve.wait_ge(ln_root, tile * SUB + q + 1)
                    dve.reciprocal(stat[:, 11:12], stat[:, 10:11]).then_inc(ln_step, 1)
                    dve.wait_ge(ln_step, k + 3)
                    stt(stat[:, 12:13], stat[:, 6:7], -1.0, stat[:, 11:12], ALU.mult, ALU.mult).then_inc(ln_step, 1)
                    dve.wait_ge(ln_step, k + 4)
                    dve.wait_ge(xT_ps, tile * SUB + q - 1 + 2)
                    dve.wait_ge(stored[q % 2], 32 * (tile * 2 + q // 2 + 1))
                    dve.tensor_scalar(x1[:, q % 2, :], xt[:, q, :], stat[:, 11:12], stat[:, 12:13], ALU.mult, ALU.add).then_inc(x1_in, 1)
                st = lambda k: tile * (H + 11) + H + k
                dve.wait_ge(logit_ps, tile * SUB + SUB + 2)
                dve.tensor_copy(L[:, :, :], bank[1][:, 0:SUB * E].rearrange("p (q e) -> p q e", q=SUB)).then_inc(route_step, 1)
                dve.wait_ge(route_step, st(1))
                dve.tensor_reduce(small[:, 0, :], L[:, :, :], X, ALU.max).then_inc(route_step, 1)
                dve.wait_ge(route_step, st(2))
                tt(L[:, :, :], L[:, :, :], small[:, 0, :].unsqueeze(2).to_broadcast([P, SUB, E]), ALU.subtract).then_inc(route_max, 1)
                dve.wait_ge(route_exp, tile + 1)
                dve.tensor_reduce(small[:, 1, :], Lp[:, :, :], X, ALU.add).then_inc(route_step, 1)
                dve.wait_ge(route_step, st(3))
                dve.reciprocal(small[:, 2, :], small[:, 1, :]).then_inc(route_step, 1)
                dve.wait_ge(route_step, st(4))
                tt(L[:, :, :], Lp[:, :, :], small[:, 2, :].unsqueeze(2).to_broadcast([P, SUB, E]), ALU.mult).then_inc(route_step, 1)
                dve.wait_ge(route_step, st(5))
                pe_, pj = (L[:, :, :].unsqueeze(u).to_broadcast([P, SUB, E, E]) for u in (3, 2))
                tt(big[:, :, :, :], pj, pe_, ALU.is_equal).then_inc(route_step, 1)
                tt(big2[:, :, :, :], pj, pe_, ALU.is_gt).then_inc(route_step, 1)
                dve.wait_ge(route_step, st(6))
                tt(big[:, :, :, :], big[:, :, :, :],
                   lower[:, :].rearrange("p (e j) -> p e j", e=E).unsqueeze(1).to_broadcast([P, SUB, E, E]),
                   ALU.mult).then_inc(route_step, 1)
                dve.wait_ge(route_step, st(8))
                tt(big[:, :, :, :], big[:, :, :, :], big2[:, :, :, :], ALU.add).then_inc(route_step, 1)
                dve.wait_ge(route_step, st(9))
                dve.tensor_reduce(Lp[:, :, :], big[:, :, :, :], X, ALU.add).then_inc(route_step, 1)
                dve.wait_ge(route_step, st(10))
                dve.tensor_scalar(Lp[:, :, :], Lp[:, :, :], 1.5, 0.5, ALU.is_lt, ALU.mult).then_inc(route_step, 1)
                dve.wait_ge(route_step, st(11))
                tt(gates_all[:, ds(tile * SUB, SUB), 0:E], L[:, :, :], Lp[:, :, :], ALU.mult).then_inc(routed, 1)


def experts(nc, io, dram, gates_all, out):
    ctx = ExitStack()
    with ctx:
        def sb(name, shape, dtype=F32):
            return ctx.enter_context(nc.sbuf_tensor(name, shape, dtype))

        def sem(name):
            return ctx.enter_context(nc.semaphore(name))

        xs = sb("e_xs", [P, 2, DC, TH], F32R)
        acc = sb("e_acc", [P, RH, D])
        w1 = [sb(f"e_w1_{i}", [P, 2, DC * FF], F32R) for i in range(2)]
        w3 = [sb(f"e_w3_{i}", [P, 2, DC * FF], F32R) for i in range(2)]
        w2 = [sb(f"e_w2_{i}", [P, 2, FB * D], F32R) for i in range(2)]
        raw = [sb(f"e_raw_{j}", [P, DC * FF]) for j in range(3)]
        g = sb("e_g", [P, 2, TT])
        hs = sb("e_hs", [P, 3, 2, TT], F32R)
        eps = sb("e_eps", [P, 1])
        one = sb("e_one", [P, 1])
        stats = sb("e_stats", [P, 2, 8])
        mean_var = sb("e_mean_var", [P, RH, 2])
        sd, rstd, shift = (sb(n, [P, RH]) for n in ("e_sd", "e_rstd", "e_shift"))
        y = sb("e_y", [P, 2, D])
        up1 = [ctx.enter_context(nc.psum_tensor(f"up1_{i}", [P, TT], F32)) for i in range(2)]
        up3 = [ctx.enter_context(nc.psum_tensor(f"up3_{i}", [P, TT], F32)) for i in range(2)]
        dn = [ctx.enter_context(nc.psum_tensor(f"dn_{i}", [P, TT], F32)) for i in range(SUB)]

        raw_in = [sem(f"e_raw_in{j}") for j in range(3)]
        split = [sem(f"e_split{j}") for j in range(3)]
        x_hi, w_hi, acc_in, set_in = sem("e_x_hi"), sem("e_w_hi"), sem("e_acc_in"), sem("e_set")
        gate_ps, up_ps, gate_in, h_in = sem("e_gate_ps"), sem("e_up_ps"), sem("e_gate_in"), sem("e_h_in")
        hi_in, lo_in = sem("e_hi_in"), sem("e_lo_in")
        down_ps, added = sem("e_down_ps"), sem("e_added")
        ln_step, root, y_in, y_out = sem("e_ln_step"), sem("e_root"), sem("e_y_in"), [sem(f"e_y_out{i}") for i in range(2)]
        block = ctx.enter_context(nc.Block())

        def expert_loop(eng, body, first=True):
            if first:
                body(0, 0)
            with eng.Fori(0, E // 2) as pair:
                body(pair * 2 + 1, 1)
                body(pair * 2 + 2, 0)

        @block.sync
        def _(sp):
            def load_x(half):
                for c in range(DC):
                    sp.wait_ge(split[c], half * (NE + 1) + 1)
                    sp.dma_start(raw[c][:, :], dram["x1T"][:, c, half * TH:(half + 1) * TH]).then_inc(raw_in[c], 16)

            def load_w(half):
                def load(e, i):
                    for j, w in enumerate(("w1", "w3", "w2")):
                        used = half * (NE + 1) + 1 + e if j < 2 else half * NE + e
                        sp.wait_ge(split[j], used + 1)
                        sp.dma_start(raw[j][:, :], io[w][:, ds(e, 1), :, :].rearrange("p o c f -> p (o c f)")).then_inc(raw_in[j], 16)
                return load

            def load_acc(half):
                sp.dma_start(acc[:, :, :], dram["x1"][:, half * RH:(half + 1) * RH, :]).then_inc(acc_in, 16)

            def store_y(half):
                with sp.Fori(0, RH // 2) as i:
                    for b in range(2):
                        sp.wait_ge(y_in, i * 2 + (half * RH + b + 1))
                        sp.dma_start(out[:, ds(i * 2 + (half * RH + b), 1), :], y[:, b:b + 1, :]).then_inc(y_out[b], 16)
            for b in range(2):
                sp.sem_inc(y_out[b], 16)
            load_x(0)
            load_acc(0)
            expert_loop(sp, load_w(0))
            load_x(1)
            load_w(1)(0, 0)
            store_y(0)
            load_acc(1)
            expert_loop(sp, load_w(1), first=False)
            store_y(1)
            for b in range(2):
                sp.wait_ge(y_out[b], 16 * (RH + 1))

        @block.gpsimd
        def _(pool):
            pool.memset(eps[:, :], EPS).then_inc(set_in, 1)
            pool.memset(gates_all[:, :, E:NE], 0.5 / E).then_inc(set_in, 1)
            pool.memset(one[:, :], 1.0).then_inc(set_in, 1)
            pool.wait_ge(set_in, 3)
            for j in range(3):
                pool.sem_inc(split[j], 1)
            with pool.Fori(0, 2) as half:
                def split_w(e, i):
                    m = half * NE + e
                    for j, w in enumerate((w1, w3, w2)):
                        loads = half * (NE + 1) + 1 + e if j < 2 else m
                        pool.wait_ge(raw_in[j], (loads + 1) * 16)
                        pool.wait_ge(down_ps, (m if isinstance(e, int) else m - 1) * (HT * FB) + 1)
                        pool.tensor_tensor(w[i][:, 0, :], raw[j][:, :], one[:, :].to_broadcast([P, DC * FF]), ALU.mult).then_inc(w_hi, 1)
                        pool.wait_ge(w_hi, m * 3 + j + 1)
                        pool.tensor_tensor(w[i][:, 1, :], raw[j][:, :], w[i][:, 0, :].bitcast(F32), ALU.subtract).then_inc(split[j], 1)
                expert_loop(pool, split_w)

        @block.tensor
        def _(pe):
            pe.sem_inc(down_ps, 1)
            with pe.Fori(0, 2) as half:
                def body(e, i):
                    with pe.Fori(0, HT) as tile:
                        n = (half * NE + e) * HT + tile
                        x_hi_t, x_lo_t = ([xs[:, part, c, ds(tile * TT, TT)] for c in range(DC)] for part in range(2))

                        def up(f):
                            pe.wait_ge(h_in, n * FB + f - 1 + 2)
                            for w, ps, done in ((w1[i], up1[f % 2], gate_ps), (w3[i], up3[f % 2], up_ps)):
                                for c in range(DC):
                                    cols = slice(c * FF + f * P, c * FF + f * P + P)
                                    pe.matmul(ps[:, :], w[:, 0, cols], x_hi_t[c], start=c == 0, stop=False)
                                    pe.matmul(ps[:, :], w[:, 0, cols], x_lo_t[c], start=False, stop=False)
                                    k = pe.matmul(ps[:, :], w[:, 1, cols], x_hi_t[c], start=False, stop=c == DC - 1)
                                k.then_inc(done, 1)

                        def down(f):
                            pe.wait_ge(lo_in, n * FB + f + 1 + 2)
                            for q in range(SUB):
                                if f == 0:
                                    pe.wait_ge(added, n * SUB + q + 1)
                                tok, cols = slice(q * P, (q + 1) * P), slice(f * D, (f + 1) * D)
                                h_hi, h_lo = hs[:, f % 3, 0, tok], hs[:, f % 3, 1, tok]
                                pe.matmul(dn[q][:, 0:D], h_hi, w2[i][:, 0, cols], start=f == 0, stop=False)
                                pe.matmul(dn[q][:, 0:D], h_hi, w2[i][:, 1, cols], start=False, stop=False)
                                k = pe.matmul(dn[q][:, 0:D], h_lo, w2[i][:, 0, cols], start=False, stop=f == FB - 1)
                            k.then_inc(down_ps, 1)
                        pe.wait_ge(split[0], half * (NE + 1) + e + 3)
                        pe.wait_ge(split[1], half * (NE + 1) + e + 3)
                        pe.wait_ge(split[2], half * NE + e + 2)
                        for f in range(FB):
                            up(f)
                            if f >= 2:
                                down(f - 2)
                        down(FB - 2)
                        down(FB - 1)
                expert_loop(pe, body)

        @block.scalar
        def _(act):
            act.wait_ge(set_in, 3)
            def split_x(half):
                for c in range(DC):
                    act.wait_ge(raw_in[c], (half * (NE + 1) + 1) * 16)
                    act.wait_ge(down_ps, half * (NE * HT * FB) + 1)
                    act.copy(xs[:, 0, c, :], raw[c][:, :]).then_inc(x_hi, 1)

            split_x(0)
            for half in range(2):
                def body(e, i):
                    with act.Fori(0, HT) as tile:
                        n = ((half * NE + e) * HT + tile) * FB
                        for f in range(FB):
                            act.wait_ge(gate_ps, n + f + 1)
                            act.wait_ge(lo_in, n + f - 1 + 2)
                            act.activation(g[:, f % 2, :], up1[f % 2][:, :], ACT.Silu).then_inc(gate_in, 1)
                            act.wait_ge(h_in, n + f + 1 + 2)
                            act.wait_ge(down_ps, n + (f - 2 if f >= 3 else 0) + 1)
                            act.copy(hs[:, f % 3, 0, :], g[:, f % 2, :]).then_inc(hi_in, 1)
                expert_loop(act, body)
                if half == 0:
                    split_x(1)
                act.wait_ge(ln_step, (half + 1) * 2 * RH + half * 2)
                act.activation(sd[:, :], mean_var[:, :, 1], ACT.Sqrt, bias=eps[:, :]).then_inc(root, 1)

        @block.vector
        def _(dve):
            dve.sem_inc(h_in, 2)
            dve.sem_inc(lo_in, 2)
            dve.sem_inc(added, SUB)
            dve.wait_ge(set_in, 3)
            def split_x(half):
                for c in range(DC):
                    dve.wait_ge(x_hi, half * DC + c + 1)
                    dve.tensor_tensor(xs[:, 1, c, :], raw[c][:, :], xs[:, 0, c, :].bitcast(F32), ALU.subtract).then_inc(split[c], 1)

            split_x(0)
            for half in range(2):
                def body(e, i):
                    with dve.Fori(0, HT) as tile:
                        m = (half * NE + e) * HT + tile
                        for f in range(FB):
                            dve.wait_ge(up_ps, m * FB + f + 1)
                            dve.wait_ge(gate_in, m * FB + f + 1)
                            dve.tensor_tensor(g[:, f % 2, :], g[:, f % 2, :], up3[f % 2][:, :], ALU.mult).then_inc(h_in, 1)
                            dve.wait_ge(hi_in, m * FB + f + 1)
                            dve.tensor_tensor(hs[:, f % 3, 1, :], g[:, f % 2, :], hs[:, f % 3, 0, :].bitcast(F32), ALU.subtract).then_inc(lo_in, 1)
                        dve.wait_ge(acc_in, half * 16 + 16)
                        dve.wait_ge(down_ps, m * FB + FB + 1)
                        for q in range(SUB):
                            dve.wait_ge(added, m * SUB + q + 1)
                            r = ds(tile * SUB + q, 1)
                            dve.scalar_tensor_tensor(acc[:, r, :].rearrange("p o d -> p (o d)"), dn[q][:, 0:D],
                                                     gates_all[:, ds(half * RH + tile * SUB + q, 1), ds(e, 1)].rearrange("p o d -> p (o d)"),
                                                     acc[:, r, :].rearrange("p o d -> p (o d)"), ALU.mult, ALU.add).then_inc(added, 1)
                expert_loop(dve, body)
                if half == 0:
                    split_x(1)
                with dve.Fori(0, RH // 2) as i:
                    for b in range(2):
                        row = acc[:, ds(i * 2 + b, 1), :].rearrange("p o d -> p (o d)")
                        dve.wait_ge(added, (half * NE + NE) * (HT * SUB) + SUB)
                        dve.bn_stats(stats[:, b, 0:6], row)
                        dve.drain()
                        dve.bn_aggr(stats[:, b, 6:8], stats[:, b, 0:6]).then_inc(ln_step, 1)
                        dve.wait_ge(ln_step, half * (2 * RH + 2) + (i * 2 + b) * 2 + 1)
                        dve.tensor_copy(mean_var[:, ds(i * 2 + b, 1), :].rearrange("p o d -> p (o d)"), stats[:, b, 6:8]).then_inc(ln_step, 1)
                k = (half + 1) * 2 * RH + half * 2
                dve.wait_ge(root, half + 1)
                dve.reciprocal(rstd[:, :], sd[:, :]).then_inc(ln_step, 1)
                dve.wait_ge(ln_step, k + 1)
                dve.scalar_tensor_tensor(shift[:, :], mean_var[:, :, 0], -1.0, rstd[:, :], ALU.mult, ALU.mult).then_inc(ln_step, 1)
                dve.drain()
                with dve.Fori(0, RH // 2) as i:
                    for b in range(2):
                        dve.wait_ge(y_out[b], half * (16 * RH // 2) + 16 * i + 16)
                        dve.tensor_scalar(y[:, b, :], acc[:, ds(i * 2 + b, 1), :].rearrange("p o d -> p (o d)"),
                                          rstd[:, ds(i * 2 + b, 1)], shift[:, ds(i * 2 + b, 1)], ALU.mult, ALU.add).then_inc(y_in, 1)


def build(nc, io, dram, out):
    gates = nc.alloc_sbuf_tensor("gates", [P, T // P, NE], F32)
    attention(nc, io, dram, gates)
    experts(nc, io, dram, gates, out)


def kernel(**inputs):
    import numpy as _np
    import concourse.bacc as _bacc
    from concourse.bass_utils import run_bass_kernel_spmd as _run

    v = {k.split("_", 2)[2] if not k.startswith("L0_ffn") else k[len("L0_ffn_"):]: _np.asarray(x)
         for k, x in inputs.items()}

    def rows(m):
        return m.reshape(-1, P, m.shape[1]).transpose(1, 0, 2)

    perm = _np.concatenate([_np.arange(h * DK, h * DK + DK) for p in range(PR) for h in (p, p + PR)])
    x = v["x"][0]
    conv = _np.concatenate([
        _np.concatenate([v[n + "_w"][:, 0, :], v[n + "_b"][:, None]], 1)[o] for n, o in
        (("qc", perm), ("kc", perm), ("vc", _np.arange(H * DV)))])
    sel_v = _np.zeros((H, H, P), _np.float32)
    sel_p = _np.zeros((H, PR, P), _np.float32)
    for h in range(H):
        sel_v[h, h] = 1.0
        sel_p[h, h % PR, 64 * (h // PR):64 * (h // PR) + 64] = 1.0
    half_ones = _np.zeros((P, 2, P), _np.float32)
    half_ones[:DK, 0] = half_ones[DK:, 1] = 1.0
    arrays = dict(
        xT=rows(x.T), x=x.reshape(-1, P, D).transpose(1, 0, 2),
        wq=rows(v["Wq"].T[:, perm]), wk=rows(v["Wk"].T[:, perm]), wv=rows(v["Wv"].T), wa=rows(v["Wa"].T),
        wg=rows(v["Wg"].T), wo=rows(v["Wo"].T), wb=rows(v["Wb"].T), gw=rows(v["gate_W"].T),
        taps=conv.reshape(16, P, KC + 1).transpose(1, 0, 2), ba=v["ba"].reshape(H, P).T, bb=v["bb"][:, None],
        lnwb=_np.stack([v["ln_w"], v["ln_b"]], 1),
        ident=_np.eye(P, dtype=_np.float32), own_pair=_np.tile(_np.repeat(_np.eye(PR, dtype=_np.float32), CH, 0), (2, 1)), half_ones=half_ones,
        mean_w=_np.full((P, P), 1.0 / P, _np.float32), sel_v=sel_v, sel_p=sel_p,
        sel_u=_np.concatenate([_np.zeros((H * CH, PR, P), _np.float32), sel_p]),
        lower=_np.broadcast_to(_np.tril(_np.ones((E, E), _np.float32), -1).reshape(1, -1), (P, E * E)),
        eps=_np.full((P, 1), EPS, _np.float32),
        w1=_np.concatenate([v["w1_e"], v["w1_s"].transpose(1, 0, 2).reshape(1, D, FF)]).reshape(NE, DC, P, FF).transpose(2, 0, 1, 3),
        w3=_np.concatenate([v["w3_e"], v["w3_s"].transpose(1, 0, 2).reshape(1, D, FF)]).reshape(NE, DC, P, FF).transpose(2, 0, 1, 3),
        w2=_np.concatenate([v["w2_e"], v["w2_s"].reshape(1, FF, D)]).reshape(NE, FB, P, D).transpose(2, 0, 1, 3),
    )
    nc = _bacc.Bacc("TRN2", target_bir_lowering=False, num_devices=1)
    feeds, io = {}, {}
    for name, arr in arrays.items():
        arr = _np.ascontiguousarray(arr)
        feeds["in_" + name] = arr
        io[name] = nc.dram_tensor("in_" + name, arr.shape, mybir.dt.from_np(arr.dtype), kind="ExternalInput").ap()
    io["const_loads"] = [n for n in arrays if n not in ("x", "xT", "w1", "w3", "w2")]
    out = nc.dram_tensor("out0", (P, T // P, D), F32, kind="ExternalOutput").ap()
    dram = dict(x1=nc.dram_tensor("x1_d", (P, T // P, D), F32, kind="Internal").ap(),
                x1T=nc.dram_tensor("x1T_d", (P, DC, T), F32, kind="Internal").ap())
    build(nc, io, dram, out)
    got = _run(nc, [feeds], core_ids=[0]).results[0]["out0"]
    return got.transpose(1, 0, 2).reshape(1, T, D)
```
